# Optimizing a Trainium2 kernel written in Bass

```python
import numpy as np
import jax
import jax.numpy as jnp

def _softmax(x, axis=-1):
    return jax.nn.softmax(x, axis=axis)

def _gelu(x):
    return jax.nn.gelu(x, approximate=True)

def _silu(x):
    return jax.nn.silu(x)

def _sigmoid(x):
    return jax.nn.sigmoid(x)

def _layernorm(x, axis=-1, eps=1e-05):
    m = jnp.mean(x, axis=axis, keepdims=True)
    v = jnp.var(x, axis=axis, keepdims=True)
    return (x - m) / jnp.sqrt(v + eps)

def _scatter_add(tgt, idx, src, axis=0):
    return tgt.at[idx].add(src)

def _segment_sum(src, seg, n):
    return jax.ops.segment_sum(src, seg, n)
kernel_name = 'mk_adj_ffn_d2_adj_r2_c0f5c0'

def setup_inputs(seed: int=0):
    np.random.seed(seed)
    _w = jnp.asarray

    def _rec_inputs():
        import jax
        import jax.numpy as jnp
        _gk = jax.random.key(seed)
        x = -0.000929 + 1 * jax.random.normal(jax.random.fold_in(_gk, 1), (2048, 128), jnp.float32)
        _w = (1.0 + jnp.arange(2048, dtype=jnp.float32)) ** (-0.5)
        _w = _w / _w.mean()
        _pij = jnp.clip(0.00390625 * _w[:, None] * _w[None, :], 0.0, 1.0)
        _a = jax.random.uniform(jax.random.fold_in(_gk, 2), (2048, 2048)) < _pij
        adj = _a.astype(jnp.int32)
        return (x, adj)
    x, adj = _rec_inputs()

    def _L0_gnn_setup():
        import jax, jax.numpy as jnp
        import numpy as np
        N, IN_C, OUT_C, H, CF = (2048, 128, 128, 8, 6)
        D = OUT_C // H
        key = jax.random.key(seed)
        ks = jax.random.split(key, 8)
        x = jax.random.normal(ks[0], (N, IN_C), dtype=jnp.float32)
        positions = jax.random.normal(ks[1], (N, 3), dtype=jnp.float32)
        curv_feats = jax.random.normal(ks[2], (N, CF), dtype=jnp.float32)
        adj = jax.random.randint(ks[3], (N, N), 0, 2, dtype=jnp.int32)
        W = jax.random.normal(ks[4], (OUT_C, IN_C), dtype=jnp.float32) * 0.05
        a_l = jax.random.normal(ks[5], (H, D), dtype=jnp.float32) * 0.1
        a_r = jax.random.normal(ks[6], (H, D), dtype=jnp.float32) * 0.1
        Wc = jax.random.normal(ks[7], (H, CF), dtype=jnp.float32) * 0.1
        gate = jnp.asarray(0.1, dtype=jnp.float32)
        return {'x': x, 'positions': positions, 'curv_feats': curv_feats, 'adj': adj, 'W': W, 'a_l': a_l, 'a_r': a_r, 'Wc': Wc, 'gate': gate}
    _L0_gnn_all = _L0_gnn_setup()
    _L0_gnn_in = {k: v for k, v in _L0_gnn_all.items() if k in ('positions', 'curv_feats', 'W', 'a_l', 'a_r', 'Wc', 'gate')}
    del _L0_gnn_all

    def _L0_ffn_setup():
        import jax, jax.numpy as jnp
        import numpy as np
        DIM = 128
        HEADS = 8
        NUM_KEYS = 128
        NUM_KV = NUM_KEYS ** 2
        PK_TOPK = 16
        FINAL_TOPK = 16
        DIM_KEY = DIM // 2
        P = 2

        def _pk(x, Wq_pk, pk_keys):
            b, n, _ = x.shape
            q = (x @ Wq_pk).reshape(b, n, P, HEADS, DIM_KEY).transpose(2, 0, 1, 3, 4)
            sim = jnp.einsum('pbnhd,pkhd->pbnhk', q, pk_keys)
            scores, idx = jax.lax.top_k(sim, PK_TOPK)
            idx0 = idx[0]
            idx1 = idx[1] * NUM_KEYS
            index = (idx0[..., :, None] + idx1[..., None, :]).reshape(b, n, HEADS, PK_TOPK * PK_TOPK)
            score = (scores[0][..., :, None] + scores[1][..., None, :]).reshape(b, n, HEADS, PK_TOPK * PK_TOPK)
            final_scores, pk_idx = jax.lax.top_k(score, FINAL_TOPK)
            final_indices = jnp.take_along_axis(index, pk_idx, axis=-1)
            final_scores = jax.nn.softmax(final_scores, axis=-1)
            return (final_scores, final_indices)
        key = jax.random.key(seed)
        ks = jax.random.split(key, 7)
        b, n = (2, 512)
        std = 0.02
        x = jax.random.normal(ks[0], (b, n, DIM), dtype=jnp.float32)
        Wq_pk = jax.random.normal(ks[1], (DIM, P * HEADS * DIM_KEY), dtype=jnp.float32) * std
        pk_keys = jax.random.normal(ks[2], (P, NUM_KEYS, HEADS, DIM_KEY), dtype=jnp.float32) * std
        Wq = jax.random.normal(ks[3], (DIM, HEADS * DIM), dtype=jnp.float32) * std
        keys_table = jax.random.normal(ks[4], (NUM_KV * HEADS, DIM), dtype=jnp.float32) * std
        values_table = jax.random.normal(ks[5], (NUM_KV * HEADS, DIM), dtype=jnp.float32) * std
        Wo = jax.random.normal(ks[6], (DIM * HEADS, DIM), dtype=jnp.float32) * std
        return {'x': x, 'Wq_pk': Wq_pk, 'pk_keys': pk_keys, 'Wq': Wq, 'keys_table': keys_table, 'values_table': values_table, 'Wo': Wo}
    _L0_ffn_all = _L0_ffn_setup()
    _L0_ffn_in = {k: v for k, v in _L0_ffn_all.items() if k in ('Wq_pk', 'pk_keys', 'Wq', 'keys_table', 'values_table', 'Wo')}
    del _L0_ffn_all

    def _L1_gnn_setup():
        import jax, jax.numpy as jnp
        import numpy as np
        N, F_IN, NHID, NHEADS, OUTDIM = (2048, 128, 128, 8, 128)
        ALPHA = 0.2
        NEG = -9000000000000000.0

        def _gat(x, adj, W_heads, a1, a2, W_out, b_out):
            Wh = jnp.einsum('nf,hfd->hnd', x, W_heads)
            s1 = jnp.einsum('hnd,hd->hn', Wh, a1)
            s2 = jnp.einsum('hnd,hd->hn', Wh, a2)
            e = s1[:, :, None] + s2[:, None, :]
            e = jnp.where(e > 0, e, ALPHA * e)
            e = jnp.where(adj[None, :, :] > 0, e, NEG)
            att = jax.nn.softmax(e, axis=-1)
            hp = jnp.einsum('hnm,hmd->hnd', att, Wh)
            hp = jax.nn.elu(hp)
            feat = jnp.transpose(hp, (1, 0, 2)).reshape(N, NHEADS * NHID)
            return feat @ W_out + b_out
        key = jax.random.key(seed)
        ks = jax.random.split(key, 7)
        x = jax.random.normal(ks[0], (N, F_IN), jnp.float32)
        adj = jax.random.randint(ks[1], (N, N), 0, 2, jnp.int32)
        W_heads = jax.random.normal(ks[2], (NHEADS, F_IN, NHID), jnp.float32) * (1.414 / np.sqrt(F_IN))
        a1 = jax.random.normal(ks[3], (NHEADS, NHID), jnp.float32) * 0.1
        a2 = jax.random.normal(ks[4], (NHEADS, NHID), jnp.float32) * 0.1
        W_out = jax.random.normal(ks[5], (NHID * NHEADS, OUTDIM), jnp.float32) * (1.0 / np.sqrt(NHID * NHEADS))
        b_out = jnp.zeros((OUTDIM,), jnp.float32)
        return {'x': x, 'adj': adj, 'W_heads': W_heads, 'a1': a1, 'a2': a2, 'W_out': W_out, 'b_out': b_out}
    _L1_gnn_all = _L1_gnn_setup()
    _L1_gnn_in = {k: v for k, v in _L1_gnn_all.items() if k in ('W_heads', 'a1', 'a2', 'W_out', 'b_out')}
    del _L1_gnn_all

    def _L1_ffn_setup():
        import jax, jax.numpy as jnp
        import numpy as np
        B, S, H, F, E, K = (8, 2048, 128, 256, 16, 2)
        EPS = 1e-05
        key = jax.random.key(seed)
        ks = jax.random.split(key, 9)
        sc = 0.02
        return {'x': jax.random.normal(ks[0], (B, S, H), dtype=jnp.float32), 'gate_w': jax.random.normal(ks[1], (H, E), dtype=jnp.float32) * sc, 'gate_b': jnp.zeros((E,), dtype=jnp.float32), 'w1': jax.random.normal(ks[2], (E, H, F), dtype=jnp.float32) * sc, 'b1': jnp.zeros((E, F), dtype=jnp.float32), 'w2': jax.random.normal(ks[3], (E, F, H), dtype=jnp.float32) * sc, 'b2': jnp.zeros((E, H), dtype=jnp.float32), 'gamma': jnp.ones((H,), dtype=jnp.float32), 'beta': jnp.zeros((H,), dtype=jnp.float32)}
    _L1_ffn_all = _L1_ffn_setup()
    _L1_ffn_in = {k: v for k, v in _L1_ffn_all.items() if k in ('gate_w', 'gate_b', 'w1', 'b1', 'w2', 'b2', 'gamma', 'beta')}
    del _L1_ffn_all
    return {'x': x, 'adj': adj, 'L0_gnn_positions': _L0_gnn_in['positions'], 'L0_gnn_curv_feats': _L0_gnn_in['curv_feats'], 'L0_gnn_W': _L0_gnn_in['W'], 'L0_gnn_a_l': _L0_gnn_in['a_l'], 'L0_gnn_a_r': _L0_gnn_in['a_r'], 'L0_gnn_Wc': _L0_gnn_in['Wc'], 'L0_gnn_gate': _L0_gnn_in['gate'], 'L0_ffn_Wq_pk': _L0_ffn_in['Wq_pk'], 'L0_ffn_pk_keys': _L0_ffn_in['pk_keys'], 'L0_ffn_Wq': _L0_ffn_in['Wq'], 'L0_ffn_keys_table': _L0_ffn_in['keys_table'], 'L0_ffn_values_table': _L0_ffn_in['values_table'], 'L0_ffn_Wo': _L0_ffn_in['Wo'], 'L1_gnn_W_heads': _L1_gnn_in['W_heads'], 'L1_gnn_a1': _L1_gnn_in['a1'], 'L1_gnn_a2': _L1_gnn_in['a2'], 'L1_gnn_W_out': _L1_gnn_in['W_out'], 'L1_gnn_b_out': _L1_gnn_in['b_out'], 'L1_ffn_gate_w': _L1_ffn_in['gate_w'], 'L1_ffn_gate_b': _L1_ffn_in['gate_b'], 'L1_ffn_w1': _L1_ffn_in['w1'], 'L1_ffn_b1': _L1_ffn_in['b1'], 'L1_ffn_w2': _L1_ffn_in['w2'], 'L1_ffn_b2': _L1_ffn_in['b2'], 'L1_ffn_gamma': _L1_ffn_in['gamma'], 'L1_ffn_beta': _L1_ffn_in['beta']}

def reference(x, adj, L0_gnn_positions, L0_gnn_curv_feats, L0_gnn_W, L0_gnn_a_l, L0_gnn_a_r, L0_gnn_Wc, L0_gnn_gate, L0_ffn_Wq_pk, L0_ffn_pk_keys, L0_ffn_Wq, L0_ffn_keys_table, L0_ffn_values_table, L0_ffn_Wo, L1_gnn_W_heads, L1_gnn_a1, L1_gnn_a2, L1_gnn_W_out, L1_gnn_b_out, L1_ffn_gate_w, L1_ffn_gate_b, L1_ffn_w1, L1_ffn_b1, L1_ffn_w2, L1_ffn_b2, L1_ffn_gamma, L1_ffn_beta):
    import jax
    import jax.numpy as jnp

    def _L0_gnn_ref(x, positions, curv_feats, adj, W, a_l, a_r, Wc, gate):
        import jax, jax.numpy as jnp
        import numpy as np
        N, IN_C, OUT_C, H, CF = (2048, 128, 128, 8, 6)
        D = OUT_C // H
        n = x.shape[0]
        h = (x @ W.T).reshape(n, H, D)
        e_l = jnp.einsum('nhd,hd->nh', h, a_l)
        e_r = jnp.einsum('nhd,hd->nh', h, a_r)
        logits = jax.nn.leaky_relu(e_l[:, None, :] + e_r[None, :, :], negative_slope=0.2)
        curv_pair = jnp.abs(curv_feats[:, None, :] - curv_feats[None, :, :])
        curv_bias = jnp.einsum('ijf,hf->ijh', curv_pair, Wc)
        logits = logits + gate * curv_bias
        mask = (adj > 0)[:, :, None]
        logits = jnp.where(mask, logits, jnp.float32(-1000000000.0))
        attn = jax.nn.softmax(logits, axis=1)
        out = jnp.einsum('ijh,jhd->ihd', attn, h)
        return out.reshape(n, H * D)

    def _L0_ffn_ref(x, Wq_pk, pk_keys, Wq, keys_table, values_table, Wo):
        import jax, jax.numpy as jnp
        import numpy as np
        DIM = 128
        HEADS = 8
        NUM_KEYS = 128
        NUM_KV = NUM_KEYS ** 2
        PK_TOPK = 16
        FINAL_TOPK = 16
        DIM_KEY = DIM // 2
        P = 2

        def _pk(x, Wq_pk, pk_keys):
            b, n, _ = x.shape
            q = (x @ Wq_pk).reshape(b, n, P, HEADS, DIM_KEY).transpose(2, 0, 1, 3, 4)
            sim = jnp.einsum('pbnhd,pkhd->pbnhk', q, pk_keys)
            scores, idx = jax.lax.top_k(sim, PK_TOPK)
            idx0 = idx[0]
            idx1 = idx[1] * NUM_KEYS
            index = (idx0[..., :, None] + idx1[..., None, :]).reshape(b, n, HEADS, PK_TOPK * PK_TOPK)
            score = (scores[0][..., :, None] + scores[1][..., None, :]).reshape(b, n, HEADS, PK_TOPK * PK_TOPK)
            final_scores, pk_idx = jax.lax.top_k(score, FINAL_TOPK)
            final_indices = jnp.take_along_axis(index, pk_idx, axis=-1)
            final_scores = jax.nn.softmax(final_scores, axis=-1)
            return (final_scores, final_indices)
        b, n, d = x.shape
        q = (x @ Wq).reshape(b, n, HEADS, DIM) * DIM ** (-0.5)
        kv_scores, indices = _pk(x, Wq_pk, pk_keys)
        offsets = jnp.arange(HEADS, dtype=indices.dtype) * NUM_KV
        ind = indices + offsets[None, None, :, None]
        k = jnp.einsum('bnhk,bnhkd->bnhd', kv_scores, keys_table[ind])
        v = jnp.einsum('bnhk,bnhkd->bnhd', kv_scores, values_table[ind])
        sim = jnp.einsum('bihd,bjhd->bhij', q, k)
        neg = -jnp.finfo(sim.dtype).max
        causal = jnp.tril(jnp.ones((n, n), dtype=bool))
        sim = jnp.where(causal, sim, neg)
        attn = jax.nn.softmax(sim, axis=-1)
        out = jnp.einsum('bhij,bjhd->bhid', attn, v)
        out = out.transpose(0, 2, 1, 3).reshape(b, n, HEADS * DIM)
        return out @ Wo

    def _L1_gnn_ref(x, adj, W_heads, a1, a2, W_out, b_out):
        import jax, jax.numpy as jnp
        import numpy as np
        N, F_IN, NHID, NHEADS, OUTDIM = (2048, 128, 128, 8, 128)
        ALPHA = 0.2
        NEG = -9000000000000000.0

        def _gat(x, adj, W_heads, a1, a2, W_out, b_out):
            Wh = jnp.einsum('nf,hfd->hnd', x, W_heads)
            s1 = jnp.einsum('hnd,hd->hn', Wh, a1)
            s2 = jnp.einsum('hnd,hd->hn', Wh, a2)
            e = s1[:, :, None] + s2[:, None, :]
            e = jnp.where(e > 0, e, ALPHA * e)
            e = jnp.where(adj[None, :, :] > 0, e, NEG)
            att = jax.nn.softmax(e, axis=-1)
            hp = jnp.einsum('hnm,hmd->hnd', att, Wh)
            hp = jax.nn.elu(hp)
            feat = jnp.transpose(hp, (1, 0, 2)).reshape(N, NHEADS * NHID)
            return feat @ W_out + b_out
        return _gat(x, adj, W_heads, a1, a2, W_out, b_out)

    def _L1_ffn_ref(x, gate_w, gate_b, w1, b1, w2, b2, gamma, beta):
        import jax, jax.numpy as jnp
        import numpy as np
        B, S, H, F, E, K = (8, 2048, 128, 256, 16, 2)
        EPS = 1e-05
        gate_logits = x @ gate_w + gate_b
        topk_vals, topk_idx = jax.lax.top_k(gate_logits, K)
        topk_w = jax.nn.softmax(topk_vals, axis=-1)
        h = jax.nn.relu(jnp.einsum('bsh,ehf->bsef', x, w1) + b1)
        expert_out = jnp.einsum('bsef,efh->bseh', h, w2) + b2
        sel = jnp.take_along_axis(expert_out, topk_idx[:, :, :, None], axis=2)
        moe = jnp.sum(topk_w[..., None] * sel, axis=2)
        y = x + moe
        mu = jnp.mean(y, axis=-1, keepdims=True)
        var = jnp.var(y, axis=-1, keepdims=True)
        return (y - mu) / jnp.sqrt(var + EPS) * gamma + beta
    x = x + _L0_gnn_ref(_layernorm(x, axis=-1), L0_gnn_positions, L0_gnn_curv_feats, adj, L0_gnn_W, L0_gnn_a_l, L0_gnn_a_r, L0_gnn_Wc, L0_gnn_gate)
    x = x + _L0_ffn_ref(_layernorm(x, axis=-1)[None], L0_ffn_Wq_pk, L0_ffn_pk_keys, L0_ffn_Wq, L0_ffn_keys_table, L0_ffn_values_table, L0_ffn_Wo)[0]
    x = x + _L1_gnn_ref(_layernorm(x, axis=-1), adj, L1_gnn_W_heads, L1_gnn_a1, L1_gnn_a2, L1_gnn_W_out, L1_gnn_b_out)
    x = x + _L1_ffn_ref(_layernorm(x, axis=-1)[None], L1_ffn_gate_w, L1_ffn_gate_b, L1_ffn_w1, L1_ffn_b1, L1_ffn_w2, L1_ffn_b2, L1_ffn_gamma, L1_ffn_beta)[0]
    return x

_drawn_inputs = setup_inputs


def setup_inputs(seed=0):
    import zlib

    import numpy as np

    out = dict(_drawn_inputs(seed))
    spreads = {'L1_gnn_b_out': (0.0, 0.1),
     'L1_ffn_gate_b': (0.0, 0.312),
     'L1_ffn_b1': (0.0, 0.8),
     'L1_ffn_b2': (0.0, 0.287),
     'L1_ffn_gamma': (1.0, 0.2),
     'L1_ffn_beta': (0.0, 0.1)}
    factors = {'L0_gnn_curv_feats': 8.0,
     'L0_gnn_a_l': 3.594,
     'L0_gnn_Wc': 8.0,
     'L0_ffn_Wq_pk': 8.0,
     'L0_ffn_pk_keys': 8.0,
     'L0_ffn_Wq': 47.533,
     'L0_ffn_keys_table': 39.737,
     'L0_ffn_values_table': 8.0,
     'L0_ffn_Wo': 8.0,
     'L1_ffn_w1': 4.157,
     'L1_ffn_w2': 3.235}
    for name, (base, spread) in spreads.items():
        noise = np.random.default_rng([zlib.crc32(name.encode()), seed]).standard_normal(out[name].shape)
        drawn = base * np.exp(spread * noise) if base else spread * noise
        out[name] = jnp.asarray(drawn.astype(out[name].dtype))
    for name, factor in factors.items():
        out[name] = (out[name] * factor).astype(out[name].dtype)
    return out
```

```python
import concourse.bass as bass
from concourse import mybir
from contextlib import ExitStack

N = 2048
C = 128
P = 128
T = N // P
H = 8
CH = 512
NC = N // CH
LN_EPS = 1e-5
MASKED = 2.0 ** 100

G = P // H
NF = 6
D0 = C // H
KC = G * NF


def program(nc, ins, out):
    fp32 = mybir.dt.float32
    bf16 = mybir.dt.bfloat16
    i32 = mybir.dt.int32
    ALU = mybir.AluOpType
    ACT = mybir.ActivationFunctionType
    X_AXIS = mybir.AxisListType.X

    with ExitStack() as whole:
        def keep(name, shape, dt):
            return whole.enter_context(nc.sbuf_tensor(name, shape, dt))

        X = keep("X", [P, T, C], fp32)
        ident = keep("ident", [P, P], fp32)
        big_ident = keep("big_ident", [P, P], bf16)
        psL = whole.enter_context(nc.psum_tensor("psL", [P, N], fp32))
        psT = whole.enter_context(nc.psum_tensor("psT", [P, 2, CH], fp32))
        psV = whole.enter_context(nc.psum_tensor("psV", [P, 4, P], fp32))
        psO = whole.enter_context(nc.psum_tensor("psO", [P, CH], fp32))

        load_rows(nc, ins, X, ident, big_ident)
        with nc.sbuf_tensor("adj_neg0", [P, T, N], bf16) as adj_neg:
            load_adjacency(nc, ins, "a0", adj_neg)
            curvature_attention(nc, ins, X, adj_neg, ident, psL, psT, psV, psO)
        with (nc.sbuf_tensor("keysT", [P, H, N], fp32) as keysT,
              nc.sbuf_tensor("values", [P, T, H, C], fp32) as values,
              nc.sbuf_tensor("xT1", [P, N], fp32) as xT):
            product_keys(nc, ins, X, xT, keysT, values, ident, psL, psT)
            causal_attention(nc, ins, X, xT, keysT, values, ident, big_ident, psL, psT, psV, psO)
        with nc.sbuf_tensor("adj_neg1", [P, T, N], bf16) as adj_neg:
            load_adjacency(nc, ins, "a1", adj_neg)
            graph_attention(nc, ins, X, adj_neg, ident, big_ident, psL, psT, psV, psO)
        experts(nc, ins, X, ident, psL, psT, psO)
        store_stage(nc, X, out)


def load_rows(nc, ins, X, ident, big_ident):
    with ExitStack() as ctx:
        rows_loaded = ctx.enter_context(nc.semaphore("rows_loaded"))
        with nc.Block() as block:
            @block.sync
            def _(sp):
                sp.dma_start(X[:, :, :], ins["x"].rearrange("(t p) c -> p t c", p=P)).then_inc(rows_loaded, 16)
                sp.dma_start(ident[:, :], ins["c_ident"]).then_inc(rows_loaded, 16)
                sp.dma_start(big_ident[:, :], ins["c_big_ident"]).then_inc(rows_loaded, 16)
                sp.wait_ge(rows_loaded, 48)


def load_adjacency(nc, ins, name, adj_neg):
    ALU = mybir.AluOpType
    SLOTS = 4
    with ExitStack() as ctx:
        raw = ctx.enter_context(nc.sbuf_tensor(name + "_adj_raw", [P, SLOTS, N], mybir.dt.int32))
        adj_loaded = [ctx.enter_context(nc.semaphore(f"{name}_adj_loaded{s}")) for s in range(SLOTS)]
        adj_turned = ctx.enter_context(nc.semaphore(name + "_adj_turned"))
        adj_v = ins["adj"].rearrange("(t p) j -> p t j", p=P)
        with nc.Block() as block:
            @block.sync
            def _(sp):
                for t in range(T):
                    if t >= SLOTS:
                        sp.wait_ge(adj_turned, t - SLOTS + 1)
                    sp.dma_start(raw[:, t % SLOTS, :], adj_v[:, t, :]).then_inc(adj_loaded[t % SLOTS], 16)

            @block.vector
            def _(dve):
                for t in range(T):
                    dve.wait_ge(adj_loaded[t % SLOTS], 16 * (t // SLOTS + 1))
                    nc.vector.tensor_scalar(adj_neg[:, t, :], raw[:, t % SLOTS, :], 0.0, -1.0,
                                            ALU.is_gt, ALU.add).then_inc(adj_turned, 1)


def store_stage(nc, X, out):
    with ExitStack() as ctx:
        stored = ctx.enter_context(nc.semaphore("stored"))
        with nc.Block() as block:
            @block.sync
            def _(sp):
                sp.dma_start(out.rearrange("(t p) c -> p t c", p=P), X[:, :, :]).then_inc(stored, 16)
                sp.wait_ge(stored, 16)


def stage_semaphores(nc, ctx, prefix):
    taken = []

    def give_back():
        nc.clear_and_free_semaphores(taken)
        nc.all_engine_barrier()

    ctx.callback(give_back)

    def sem(name):
        taken.append(nc.alloc_semaphore(prefix + name))
        return taken[-1]

    return sem


class Norm:

    def __init__(self, nc, ctx, name, X, xT, xn, ident, psT):
        def sb(what, shape):
            return ctx.enter_context(nc.sbuf_tensor(f"{name}_{what}", shape, mybir.dt.float32))

        def sem(what):
            return ctx.enter_context(nc.semaphore(f"{name}_{what}"))

        self.nc, self.X, self.xT, self.ident, self.psT = nc, X, xT, ident, psT
        self.stats = sb("stats", [P, T, 6])
        self.mv = sb("mv", [P, T, 2])
        self.eps = sb("eps", [P, 1])
        self.std = sb("std", [P, T])
        self.rstd = sb("rstd", [P, T])
        self.xn = xn
        self.stats_done = sem("stats_done")
        self.moments = sem("moments")
        self.std_done = sem("std_done")
        self.rstd_done = sem("rstd_done")
        self.xn_done = sem("xn_done")
        self.turned = sem("turned")
        self.xT_done = sem("xT_done")

    def vector(self, dve):
        nc = self.nc
        nc.vector.memset(self.eps[:, :], LN_EPS)
        for t in range(T):
            last = nc.vector.bn_stats(self.stats[:, t, :], self.X[:, t, :])
        last.then_inc(self.stats_done, 1)
        dve.wait_ge(self.stats_done, 1)
        for t in range(T):
            last = nc.vector.bn_aggr(self.mv[:, t, :], self.stats[:, t, :])
        last.then_inc(self.moments, 1)
        dve.wait_ge(self.std_done, 1)
        nc.vector.reciprocal(self.rstd[:, :], self.std[:, :]).then_inc(self.rstd_done, 1)
        dve.wait_ge(self.rstd_done, 1)
        for t in range(T):
            nc.vector.tensor_scalar(self.xn[:, t, :], self.X[:, t, :], self.mv[:, t, 0:1], self.rstd[:, t:t + 1],
                                    mybir.AluOpType.subtract, mybir.AluOpType.mult).then_inc(self.xn_done, 1)

    def scalar(self, act):
        nc = self.nc
        act.wait_ge(self.moments, 1)
        nc.scalar.activation(self.std[:, :], self.mv[:, :, 1], mybir.ActivationFunctionType.Sqrt,
                             bias=self.eps[:, :]).then_inc(self.std_done, 1)
        for q in range(T // 4):
            act.wait_ge(self.turned, q + 1)
            nc.scalar.copy(self.xT[:, 4 * q * P:4 * (q + 1) * P], self.psT[:, q % 2, :]).then_inc(self.xT_done, 1)

    def tensor(self, pe):
        nc = self.nc
        for t in range(T):
            q = t // 4
            if t % 4 == 0 and q >= 2:
                pe.wait_ge(self.xT_done, q - 1)
            pe.wait_ge(self.xn_done, t + 1)
            last = nc.tensor.transpose(self.psT[:, q % 2, (t % 4) * P:(t % 4 + 1) * P], self.xn[:, t, :],
                                       self.ident[:, :])
            if t % 4 == 3:
                last.then_inc(self.turned, 1)


def curvature_attention(nc, ins, X, adj_neg, ident, psL, psT, psV, psO):
    fp32 = mybir.dt.float32
    bf16 = mybir.dt.bfloat16
    ALU = mybir.AluOpType
    ACT = mybir.ActivationFunctionType
    SLOPE = 0.2
    UNITS = N // G
    KU = UNITS // T
    KW = KC + NF
    KB = KW + H
    with ExitStack() as ctx:
        def sb(name, shape, dt=fp32):
            return ctx.enter_context(nc.sbuf_tensor("ca_" + name, shape, dt))

        sem = stage_semaphores(nc, ctx, "ca_")

        vals = sb("vals", [P, T, C])
        er_rows = sb("er_rows", [P, N])
        el_cols = sb("el_cols", [P, UNITS])
        c_cols = sb("c_cols", [KC, UNITS])
        c_rows = sb("c_rows", [KC, N])
        bias_rhs = sb("bias_rhs", [KB, 2, N])
        bias_w = sb("bias_w", [KB, P])
        spread = sb("spread", [P, KU, P], bf16)
        fold = sb("fold", [P, KU, P])
        own_head = sb("own_head", [P, P])
        relu_part = sb("relu_part", [P, 2, N])
        logits = sb("logits", [P, 2, N])
        probs = sb("probs", [P, 2, N])
        probsT = sb("probsT", [P, T, P])
        mx = sb("mx", [P, 2])
        waited = sb("waited", [P, 1])
        neg_mx = sb("neg_mx", [P, 2])
        rsum = sb("rsum", [P, 2])
        rinv = sb("rinv", [P, 2])
        picked = sb("picked", [P, 2, P])
        node_pick = ctx.enter_context(nc.sbuf_tensor("ca_node_pick", [P, G], fp32))
        xT = logits[:, 0, :]
        hT = logits[:, 1, :]
        el_wide = probs[:, 0, :]
        w_t = probs[:, 1, 0:P]
        al_w = probs[:, 1, P:2 * P]
        ar_w = probs[:, 1, 2 * P:3 * P]
        head_mask = probs[:, 1, 3 * P:4 * P]
        al_col = probs[:, 1, 4 * P:4 * P + 1]
        ar_col = probs[:, 1, 4 * P + 1:4 * P + 2]
        wc_raw = probs[0:KW, 1, 5 * P:6 * P]
        bias_mask = probs[0:KW, 1, 6 * P:7 * P]
        gate_col = probs[0:KW, 1, 7 * P:7 * P + 1]
        norm = Norm(nc, ctx, "ca_norm", X, xT, probsT, ident, psT)

        consts_in = sem("consts_in")
        mats_in = sem("mats_in")
        weights_ready = sem("weights_ready")
        prep_mm = sem("prep_mm")
        prep_copied = sem("prep_copied")
        er8_in = sem("er8_in")
        cols_ready = sem("cols_ready")
        el_mult = sem("el_mult")
        bias_ready = sem("bias_ready")
        diff_ready = sem("diff_ready")
        relu_ready = sem("relu_ready")
        logits_ready = sem("logits_ready")
        mx_found = sem("mx_found")
        mx_ready = sem("mx_ready")
        probs_ready = sem("probs_ready")
        turned = sem("turned")
        probsT_ready = sem("probsT_ready")
        pv_ready = sem("pv_ready")
        rinv_ready = sem("rinv_ready")
        picked_ready = sem("picked_ready")
        folded = sem("folded")
        x_added = sem("x_added")

        with nc.Block() as block:
            @block.sync
            def _(sp):
                with nc.allow_non_contiguous_dma(reason="small weights"):
                    sp.dma_start(w_t, ins["W_t"]).then_inc(mats_in, 16)
                    sp.dma_start(al_col, ins["a_l"]).then_inc(mats_in, 16)
                    sp.dma_start(ar_col, ins["a_r"]).then_inc(mats_in, 16)
                    sp.dma_start(head_mask, ins["c_head_mask"]).then_inc(mats_in, 16)
                    sp.dma_start(bias_mask, ins["c_bias_mask"]).then_inc(mats_in, 16)
                    sp.dma_start(wc_raw, ins["wc_tiled"]).then_inc(mats_in, 16)
                    sp.dma_start(gate_col, ins["gate"].to_broadcast([KW, 1])).then_inc(mats_in, 16)
                    for i in range(G):
                        sp.dma_start(c_rows[i * NF:(i + 1) * NF, :], ins["curv_t"]).then_inc(consts_in, 16)
                    sp.dma_start(bias_w[KW:KB, :], ins["c_slope_rows"]).then_inc(consts_in, 16)
                    for b in range(2):
                        sp.dma_start(bias_rhs[KC:KW, b, :], ins["curv_t"]).then_inc(consts_in, 16)
                    sp.dma_start(c_cols[:, :], ins["curv_cols"]).then_inc(consts_in, 16)
                    sp.dma_start(spread[:, :, :], ins["c_spread"]).then_inc(consts_in, 16)
                    sp.dma_start(fold[:, :, :], ins["c_fold"]).then_inc(consts_in, 16)
                    sp.dma_start(own_head[:, :], ins["c_own_head"]).then_inc(consts_in, 16)
                    sp.dma_start(node_pick[:, :], ins["c_node_pick"]).then_inc(consts_in, 16)
                sp.wait_ge(prep_copied, 13)
                for b in range(2):
                    sp.dma_start(bias_rhs[KW:KB, b, :], er_rows[0:H, :]).then_inc(er8_in, 16)

            @block.tensor
            def _(pe):
                norm.tensor(pe)
                pe.wait_ge(norm.xT_done, T // 4)
                pe.wait_ge(mats_in, 16 * 7)
                for c in range(NC):
                    nc.tensor.matmul(psL[:, c * CH:(c + 1) * CH], w_t, xT[:, c * CH:(c + 1) * CH],
                                     start=True, stop=True).then_inc(prep_mm, 1)
                for q in range(4):
                    if q == 0:
                        pe.wait_ge(prep_copied, 4)
                    else:
                        pe.wait_ge(prep_copied, 4 + q)
                    for s in range(4):
                        t = 4 * q + s
                        last = nc.tensor.matmul(psT[:, q % 2, s * P:(s + 1) * P], xT[:, t * P:(t + 1) * P], w_t,
                                                start=True, stop=True)
                    last.then_inc(prep_mm, 1)
                pe.wait_ge(weights_ready, 2)
                pe.wait_ge(prep_copied, 8)
                for c in range(NC):
                    nc.tensor.matmul(psL[:, c * CH:(c + 1) * CH], al_w, hT[:, c * CH:(c + 1) * CH],
                                     start=True, stop=True).then_inc(prep_mm, 1)
                for c in range(NC):
                    pe.wait_ge(prep_copied, 9 + c)
                    nc.tensor.matmul(psL[:, c * CH:(c + 1) * CH], ar_w, hT[:, c * CH:(c + 1) * CH],
                                     start=True, stop=True).then_inc(prep_mm, 1)

                def logits_of(t, k, first=False):
                    u = KU * t + k
                    for c in range(NC):
                        if c == 0 and not first:
                            pe.wait_ge(mx_ready, u)
                        nc.tensor.matmul(psL[:, c * CH:(c + 1) * CH], spread[:, k, :],
                                         adj_neg[:, t, c * CH:(c + 1) * CH], start=True, stop=False)
                        if c == 0:
                            pe.wait_ge(diff_ready, u + 1)
                        last = nc.tensor.matmul(psL[:, c * CH:(c + 1) * CH], bias_w[:, :],
                                                bias_rhs[:, k % 2, c * CH:(c + 1) * CH], start=False, stop=True)
                    last.then_inc(logits_ready, 1)

                def turn(k, q):
                    for s in range(4):
                        j = 4 * q + s
                        last = nc.tensor.transpose(psT[:, q % 2, s * P:(s + 1) * P],
                                                   probs[:, k % 2, j * P:(j + 1) * P], ident[:, :])
                    last.then_inc(turned, 1)

                def weigh(t, k, q):
                    u = KU * t + k
                    pe.wait_ge(probsT_ready, 4 * u + q + 1)
                    for s in range(4):
                        j = 4 * q + s
                        last = nc.tensor.matmul(psV[:, k % 2, :], probsT[:, j, :], vals[:, j, :],
                                                start=(j == 0), stop=(j == T - 1))
                    if q == 3:
                        last.then_inc(pv_ready, 1)

                def fold_in(t, k):
                    pe.wait_ge(picked_ready, KU * t + k + 1)
                    last = nc.tensor.matmul(psO[:, 0:P], fold[:, k, :], picked[:, k % 2, :],
                                            start=(k == 0), stop=(k == KU - 1))
                    if k == KU - 1:
                        last.then_inc(folded, 1)

                def tile_of_units(t, last):
                    for k in range(KU):
                        if k < KU - 1:
                            logits_of(t, k + 1)
                        elif not last:
                            logits_of(t + 1, 0)
                        if k >= 1:
                            fold_in(t, k - 1)
                        pe.wait_ge(probs_ready, KU * t + k + 1)
                        turn(k, 0)
                        turn(k, 1)
                        weigh(t, k, 0)
                        turn(k, 2)
                        weigh(t, k, 1)
                        turn(k, 3)
                        weigh(t, k, 2)
                        weigh(t, k, 3)
                    fold_in(t, KU - 1)

                pe.wait_ge(consts_in, 16 * (G + 8))
                pe.wait_ge(bias_ready, 1)
                pe.wait_ge(er8_in, 32)
                pe.wait_ge(prep_copied, 16)
                logits_of(0, 0, first=True)
                with pe.Fori(0, T - 1) as t:
                    tile_of_units(t, False)
                tile_of_units(T - 1, True)

            @block.scalar
            def _(act):
                norm.scalar(act)
                for c in range(NC):
                    act.wait_ge(prep_mm, c + 1)
                    nc.scalar.copy(hT[:, c * CH:(c + 1) * CH], psL[:, c * CH:(c + 1) * CH]).then_inc(prep_copied, 1)
                for q in range(4):
                    act.wait_ge(prep_mm, 4 + q + 1)
                    nc.scalar.copy(vals[:, 4 * q:4 * q + 4, :].rearrange("p s c -> p (s c)"),
                                   psT[:, q % 2, :]).then_inc(prep_copied, 1)
                for c in range(NC):
                    act.wait_ge(prep_mm, 8 + c + 1)
                    nc.scalar.mul(el_wide[:, c * CH:(c + 1) * CH], psL[:, c * CH:(c + 1) * CH],
                                  1.0 - SLOPE).then_inc(prep_copied, 1)
                act.wait_ge(prep_mm, 16)
                nc.scalar.copy(er_rows[:, :], psL[:, :]).then_inc(prep_copied, 4)
                act.wait_ge(cols_ready, 1)
                act.wait_ge(prep_copied, 16)

                def relu_of(t, k):
                    u = KU * t + k
                    nc.scalar.activation(relu_part[:, k % 2, :], er_rows[:, :], ACT.Relu,
                                         bias=el_cols[:, bass.ds(u, 1)], scale=1.0 - SLOPE).then_inc(relu_ready, 1)

                def exp_of(t, k):
                    act.wait_ge(mx_ready, KU * t + k + 1)
                    nc.scalar.activation(probs[:, k % 2, :], logits[:, k % 2, :], ACT.Exp,
                                         bias=neg_mx[:, k % 2:k % 2 + 1],
                                         accum_out=rsum[:, k % 2:k % 2 + 1]).then_inc(probs_ready, 1)

                def copy_turned(t, k):
                    for q in range(4):
                        act.wait_ge(turned, 4 * (KU * t + k) + q + 1)
                        nc.scalar.copy(probsT[:, 4 * q:4 * q + 4, :].rearrange("p s c -> p (s c)"),
                                       psT[:, q % 2, :]).then_inc(probsT_ready, 1)

                def tile_of_units(t, last):
                    for k in range(KU):
                        if k < KU - 2 or not last:
                            relu_of(t, k + 2) 
                        copy_turned(t, k)
                        if k < KU - 1 or not last:
                            exp_of(t + (k + 1) // KU, (k + 1) % KU)

                relu_of(0, 0)
                relu_of(0, 1)
                exp_of(0, 0)
                with act.Fori(0, T - 1) as t:
                    tile_of_units(t, False)
                tile_of_units(T - 1, True)

            @block.vector
            def _(dve):
                norm.vector(dve)
                dve.wait_ge(mats_in, 16 * 7)
                nc.vector.tensor_scalar(al_w, head_mask, al_col, None, ALU.mult).then_inc(weights_ready, 1)
                nc.vector.tensor_scalar(ar_w, head_mask, ar_col, None, ALU.mult).then_inc(weights_ready, 1)
                nc.vector.scalar_tensor_tensor(bias_w[0:KW, :], wc_raw, gate_col, bias_mask,
                                               ALU.mult, ALU.mult).then_inc(bias_ready, 1)
                dve.wait_ge(consts_in, 16 * (G + 8))
                dve.wait_ge(prep_copied, 12)
                nc.vector.tensor_tensor(probs[:, 0, :].rearrange("p (u i) -> p u i", i=G),
                                        el_wide.rearrange("p (u i) -> p u i", i=G),
                                        node_pick[:, :].unsqueeze(1).to_broadcast([P, UNITS, G]),
                                        ALU.mult).then_inc(el_mult, 1)
                dve.wait_ge(el_mult, 1)
                nc.vector.tensor_reduce(el_cols[:, :], probs[:, 0, :].rearrange("p (u i) -> p u i", i=G),
                                        mybir.AxisListType.X, ALU.add).then_inc(cols_ready, 1)

                def diff_of(t, k):
                    u = KU * t + k
                    nc.vector.tensor_scalar(bias_rhs[0:KC, k % 2, :], c_rows[:, :], c_cols[:, bass.ds(u, 1)], 0.0,
                                            ALU.subtract, ALU.max).then_inc(diff_ready, 1)

                def max_of(t, k):
                    u = KU * t + k
                    dve.wait_ge(relu_ready, u + 1)
                    dve.wait_ge(logits_ready, u + 1)
                    nc.vector.memset(waited[:, :], 0.0)
                    nc.vector.tensor_tensor_reduce(out=logits[:, k % 2, :], in0=psL[:, :], in1=relu_part[:, k % 2, :],
                                                   scale=1.0, scalar=-3.0e38, op0=ALU.add, op1=ALU.max,
                                                   accum_out=mx[:, k % 2:k % 2 + 1]).then_inc(mx_found, 1)
                    dve.wait_ge(mx_found, u + 1)
                    nc.vector.tensor_scalar(neg_mx[:, k % 2:k % 2 + 1], mx[:, k % 2:k % 2 + 1], -1.0, None,
                                            ALU.mult).then_inc(mx_ready, 1)

                def pick(t, k):
                    u = KU * t + k
                    dve.wait_ge(pv_ready, u + 1)
                    nc.vector.reciprocal(rinv[:, k % 2:k % 2 + 1], rsum[:, k % 2:k % 2 + 1]).then_inc(rinv_ready, 1)
                    dve.wait_ge(rinv_ready, u + 1)
                    nc.vector.scalar_tensor_tensor(picked[:, k % 2, :], psV[:, k % 2, :], rinv[:, k % 2:k % 2 + 1],
                                                   own_head[:, :], ALU.mult, ALU.mult).then_inc(picked_ready, 1)

                def tile_of_units(t, last):
                    for k in range(KU):
                        if k < KU - 2 or not last:
                            diff_of(t, k + 2)
                        if k < KU - 1 or not last:
                            max_of(t + (k + 1) // KU, (k + 1) % KU)
                        pick(t, k)
                    dve.wait_ge(folded, t + 1)
                    nc.vector.tensor_tensor(X[:, t, :], X[:, t, :], psO[:, 0:P], ALU.add).then_inc(x_added, 1)

                diff_of(0, 0)
                diff_of(0, 1)
                max_of(0, 0)
                with dve.Fori(0, T - 1) as t:
                    tile_of_units(t, False)
                tile_of_units(T - 1, True)


class Chain:

    def __init__(self, engine, semaphore):
        self.engine, self.semaphore, self.count = engine, semaphore, 0

    def did(self, instruction):
        instruction.then_inc(self.semaphore, 1)
        self.count += 1
        return self.count

    def restart(self):
        self.engine.wait_ge(self.semaphore, self.count)
        self.engine.sem_clear(self.semaphore)
        self.count = 0


NK = 128
DK = C // 2
TOP = 16
RUNS = [(0, 1, 16), (1, 1, 8), (2, 1, 5), (3, 1, 4), (4, 1, 3), (5, 3, 2), (8, 8, 1)]
CAND = sum(rows * cols for _, rows, cols in RUNS)
RING = 2 * TOP


def product_keys(nc, ins, X, xT, keysT, values, ident, psL, psT):
    fp32 = mybir.dt.float32
    u32 = mybir.dt.uint32
    ALU = mybir.AluOpType
    ACT = mybir.ActivationFunctionType
    LOWEST = -3.0e38
    with ExitStack() as ctx:
        def sb(name, shape, dt=fp32):
            return ctx.enter_context(nc.sbuf_tensor("pk_" + name, shape, dt))

        sem = stage_semaphores(nc, ctx, "pk_")

        wq = sb("wq", [P, H, P])
        keys = sb("keys", [P, H, 2 * NK])
        cand_no = sb("cand_no", [P, CAND])
        qT = sb("qT", [P, 2, P])
        sim = sb("sim", [P, 2, 2, NK])
        rest = sb("rest", [P, 2, NK])
        best = sb("best", [P, 2, TOP])
        best_at = sb("best_at", [P, 2, TOP], u32)
        at0 = sb("at0", [P, TOP])
        at1 = sb("at1", [P, TOP])
        cand = sb("cand", [P, CAND])
        cand_rest = sb("cand_rest", [P, CAND])
        cand_row = sb("cand_row", [P, CAND])
        top = sb("top", [P, TOP])
        top_at = sb("top_at", [P, TOP], u32)
        hit = sb("hit", [P, TOP, CAND])
        neg_top = sb("neg_top", [P, 1])
        raw_w = sb("raw_w", [P, H, TOP])
        sum_w = sb("sum_w", [P, H])
        inv_w = sb("inv_w", [P, H])
        rows = sb("rows", [P, H, TOP], u32)
        ring = sb("ring", [P, RING, 2 * C])
        norm = Norm(nc, ctx, "pk_norm", X, xT, ring[:, 0:T // 2, :].rearrange("p a (b c) -> p (a b) c", c=C),
                    ident, psT)
        part = sb("part", [P, 2, 2, 2 * C])
        total = sb("total", [P, 2, C])

        def qT_ps(k):
            return psL[:, (k % 2) * CH:(k % 2) * CH + P]

        def key_ps(k):
            return psL[:, (2 + k % 2) * CH:(2 + k % 2) * CH + P]

        consts_in = sem("consts_in")
        keys_zeroed = sem("keys_zeroed")
        qT_done = sem("qT_done")
        qT_copied = sem("qT_copied")
        sim_done = sem("sim_done")
        sim_copied = sem("sim_copied")
        sim_seen = sem("sim_seen")
        sim_free = sem("sim_free")
        top_ready = sem("top_ready")
        exp_ready = sem("exp_ready")
        rows_ready = sem("rows_ready")
        rows_seen = sem("rows_seen")
        ring_free = sem("ring_free")
        ring_seen = sem("ring_seen")
        got = [sem(f"got{i}") for i in range(RING)]
        step = sem("step")
        total_ready = sem("total_ready")
        key_turned = sem("key_turned")
        key_seen = sem("key_seen")
        key_copied = sem("key_copied")

        with nc.Block() as block:
            @block.sync
            def _(sp):
                sp.dma_start(wq[:, :, :], ins["Wq_pk"]).then_inc(consts_in, 16)
                sp.dma_start(cand_no[:, :], ins["c_cand_no"]).then_inc(consts_in, 16)
                sp.wait_ge(keys_zeroed, 1)
                for p in range(2):
                    sp.dma_start(keys[p * DK:(p + 1) * DK, :, p * NK:(p + 1) * NK],
                                 ins["pk_keys"][p, :, :, :]).then_inc(consts_in, 16)

            @block.gpsimd
            def _(pool):
                def gather(t, k):
                    u = H * t + k
                    pool.wait_ge(rows_ready, u + 1)
                    pool.sem_inc(rows_seen, 1)
                    pool.wait_ge(ring_free, u + 1)
                    pool.sem_inc(ring_seen, 1)
                    for s in range(TOP):
                        slot = (k % 2) * TOP + s
                        pool.indirect_dma_start(ring[:, slot, :], None, ins["tables"],
                                                bass.IndirectOffsetOnAxis(rows[:, k, s:s + 1], axis=0)
                                                ).then_inc(got[slot], 16)

                with pool.Fori(0, T) as t:
                    for k in range(H):
                        gather(t, k)

            @block.tensor
            def _(pe):
                norm.tensor(pe)
                pe.wait_ge(norm.xT_done, T // 4)
                pe.wait_ge(consts_in, 64)

                def similarity(t, k):
                    v = H * t + k
                    nc.tensor.matmul(qT_ps(k), wq[:, k, :], xT[:, bass.ts(t, P)],
                                     start=True, stop=True).then_inc(qT_done, 1)
                    pe.wait_ge(qT_copied, v + 1)
                    nc.tensor.matmul(psT[:, k % 2, 0:2 * NK], qT[:, k % 2, :], keys[:, k, :],
                                     start=True, stop=True).then_inc(sim_done, 1)

                def turn_key(t, k):
                    pe.wait_ge(total_ready, H * t + k + 1)
                    nc.tensor.transpose(key_ps(k), total[:, k % 2, :], ident[:, :]).then_inc(key_turned, 1)

                for k in range(H):
                    similarity(0, k)
                with pe.Fori(0, T - 1) as t:
                    for k in range(H):
                        similarity(t + 1, k)
                        turn_key(t, k)
                for k in range(H):
                    pe.wait_ge(key_copied, H * (T - 1) + k - 1)
                    turn_key(T - 1, k)

            @block.scalar
            def _(act):
                norm.scalar(act)

                def similarity(t, k):
                    v = H * t + k
                    act.wait_ge(qT_done, v + 1)
                    nc.scalar.copy(qT[:, k % 2, :], qT_ps(k)).then_inc(qT_copied, 1)
                    act.wait_ge(sim_done, v + 1)
                    act.wait_ge(sim_free, v + 1)
                    nc.scalar.copy(sim[:, k % 2, :, :].rearrange("p a b -> p (a b)"),
                                   psT[:, k % 2, 0:2 * NK]).then_inc(sim_copied, 1)
                    act.wait_ge(top_ready, v + 1)
                    nc.scalar.activation(raw_w[:, k, :], top[:, :], ACT.Exp, bias=neg_top[:, :],
                                         accum_out=sum_w[:, k:k + 1]).then_inc(exp_ready, 1)

                def keep_key(t, k):
                    act.wait_ge(key_turned, H * t + k + 1)
                    act.sem_inc(key_seen, 1)
                    nc.scalar.copy(keysT[:, k, bass.ts(t, P)], key_ps(k)).then_inc(key_copied, 1)

                for k in range(H):
                    similarity(0, k)
                with act.Fori(0, T - 1) as t:
                    for k in range(H):
                        similarity(t + 1, k)
                        keep_key(t, k)
                for k in range(H):
                    keep_key(T - 1, k)

            @block.vector
            def _(dve):
                norm.vector(dve)
                nc.vector.memset(keys[:, :, :], 0.0).then_inc(keys_zeroed, 1)
                dve.sem_inc(sim_free, 2)
                dve.sem_inc(ring_free, 2)
                dve.wait_ge(consts_in, 64)
                c = Chain(dve, step)

                def choose(t, k):
                    v = H * t + k
                    dve.wait_ge(sim_copied, v + 1)
                    dve.sem_inc(sim_seen, 1)
                    s = sim[:, k % 2, :, :]
                    first = [c.did(nc.vector.max(best[:, p, 0:8], s[:, p, :])) for p in range(2)]
                    removed = []
                    for p in range(2):
                        dve.wait_ge(step, first[p])
                        removed.append(c.did(nc.vector.match_replace(rest[:, p, :], best[:, p, 0:8], s[:, p, :],
                                                                     LOWEST)))
                    for p in range(2):
                        c.did(nc.vector.max_index(best_at[:, p, 0:8], best[:, p, 0:8], s[:, p, :]))
                    second = []
                    for p in range(2):
                        dve.wait_ge(step, removed[p])
                        second.append(c.did(nc.vector.max(best[:, p, 8:16], rest[:, p, :])))
                    for p in range(2):
                        dve.wait_ge(step, second[p])
                        found = c.did(nc.vector.max_index(best_at[:, p, 8:16], best[:, p, 8:16], rest[:, p, :]))
                    at = 0
                    spans = []
                    for i, n, m in RUNS:
                        spans.append((at, i, n, m))
                        at += n * m
                    for at, i, n, m in spans:
                        summed = c.did(nc.vector.tensor_tensor(
                            cand[:, at:at + n * m].rearrange("p (a b) -> p a b", b=m),
                            best[:, 0, i:i + n].unsqueeze(2).to_broadcast([P, n, m]),
                            best[:, 1, 0:m].unsqueeze(1).to_broadcast([P, n, m]), ALU.add))
                    dve.wait_ge(step, found)
                    c.did(nc.vector.tensor_scalar(at0[:, :], best_at[:, 0, :], float(k * NK * NK), None, ALU.add))
                    placed = c.did(nc.vector.tensor_scalar(at1[:, :], best_at[:, 1, :], float(NK), None, ALU.mult))
                    dve.wait_ge(step, summed)
                    t1 = c.did(nc.vector.max(top[:, 0:8], cand[:, :]))
                    dve.wait_ge(step, placed)
                    for at, i, n, m in spans:
                        numbered = c.did(nc.vector.tensor_tensor(
                            cand_row[:, at:at + n * m].rearrange("p (a b) -> p a b", b=m),
                            at0[:, i:i + n].unsqueeze(2).to_broadcast([P, n, m]),
                            at1[:, 0:m].unsqueeze(1).to_broadcast([P, n, m]), ALU.add))
                    dve.wait_ge(step, t1)
                    t2 = c.did(nc.vector.match_replace(cand_rest[:, :], top[:, 0:8], cand[:, :], LOWEST))
                    c.did(nc.vector.max_index(top_at[:, 0:8], top[:, 0:8], cand[:, :]))
                    dve.wait_ge(step, t2)
                    t3 = c.did(nc.vector.max(top[:, 8:16], cand_rest[:, :]))
                    dve.wait_ge(step, t3)
                    nc.vector.tensor_scalar(neg_top[:, :], top[:, 0:1], -1.0, None, ALU.mult).then_inc(top_ready, 1)
                    t4 = c.did(nc.vector.max_index(top_at[:, 8:16], top[:, 8:16], cand_rest[:, :]))
                    dve.wait_ge(step, t4)
                    t5 = c.did(nc.vector.tensor_tensor(hit[:, :, :],
                                                       top_at[:, :].unsqueeze(2).to_broadcast([P, TOP, CAND]),
                                                       cand_no[:, :].unsqueeze(1).to_broadcast([P, TOP, CAND]),
                                                       ALU.is_equal))
                    dve.wait_ge(step, t5)
                    t6 = c.did(nc.vector.tensor_tensor(hit[:, :, :], hit[:, :, :],
                                                       cand_row[:, :].unsqueeze(1).to_broadcast([P, TOP, CAND]),
                                                       ALU.mult))
                    dve.wait_ge(step, t6)
                    with nc.allow_low_precision(reason="whole numbers below 2**24, one of them not zero"):
                        c.did(nc.vector.tensor_reduce(rows[:, k, :], hit[:, :, :], mybir.AxisListType.X, ALU.add))
                    c.restart()
                    dve.sem_inc(rows_ready, 1)
                    dve.sem_inc(sim_free, 1)
                    dve.wait_ge(exp_ready, v + 1)
                    n1 = c.did(nc.vector.reciprocal(inv_w[:, k:k + 1], sum_w[:, k:k + 1]))
                    c.restart()

                def add_up(t, k, last=False):
                    u = H * t + k
                    done = []
                    for s in range(TOP):
                        slot = (k % 2) * TOP + s
                        dve.wait_ge(got[slot], 16 * ((H // 2) * t + k // 2 + 1))
                        if s >= 2:
                            dve.wait_ge(step, done[s - 2])
                            done.append(c.did(nc.vector.scalar_tensor_tensor(
                                part[:, k % 2, s % 2, :], ring[:, slot, :], raw_w[:, k, s:s + 1],
                                part[:, k % 2, s % 2, :], ALU.mult, ALU.add)))
                        else:
                            done.append(c.did(nc.vector.tensor_scalar(
                                part[:, k % 2, s % 2, :], ring[:, slot, :], raw_w[:, k, s:s + 1], None, ALU.mult)))
                    dve.wait_ge(step, done[TOP - 1])
                    both = c.did(nc.vector.tensor_tensor(part[:, k % 2, 0, :], part[:, k % 2, 0, :],
                                                         part[:, k % 2, 1, :], ALU.add))
                    dve.wait_ge(step, both)
                    if last:
                        dve.wait_ge(key_turned, u - 1)
                    c.did(nc.vector.tensor_scalar(total[:, k % 2, :], part[:, k % 2, 0, 0:C], inv_w[:, k:k + 1], None,
                                                  ALU.mult))
                    c.did(nc.vector.tensor_scalar(values[:, t, k, :], part[:, k % 2, 0, C:2 * C], inv_w[:, k:k + 1],
                                                  None, ALU.mult))
                    c.restart()
                    dve.sem_inc(total_ready, 1)
                    dve.sem_inc(ring_free, 1)

                for k in range(H):
                    choose(0, k)
                with dve.Fori(0, T - 1) as t:
                    for k in range(H):
                        add_up(t, k)
                        choose(t + 1, k)
                for k in range(H):
                    add_up(T - 1, k, last=True)


def causal_attention(nc, ins, X, xT, keysT, values, ident, big_ident, psL, psT, psV, psO):
    fp32 = mybir.dt.float32
    bf16 = mybir.dt.bfloat16
    ALU = mybir.AluOpType
    ACT = mybir.ActivationFunctionType
    TC = CH // P
    with ExitStack() as ctx:
        def sb(name, shape, dt=fp32):
            return ctx.enter_context(nc.sbuf_tensor("at_" + name, shape, dt))

        sem = stage_semaphores(nc, ctx, "at_")

        wq = sb("wq", [P, H, C])
        wo = sb("wo", [P, H, C])
        ahead = sb("ahead", [P, TC, CH], bf16)
        qT = sb("qT", [P, H, P])
        probs = sb("probs", [P, 2, N])
        probsT = sb("probsT", [P, T, P])
        neg_mx = sb("neg_mx", [P, 2])
        rsum = sb("rsum", [P, 2])
        rinv = sb("rinv", [P, 2])
        headT = sb("headT", [P, 2, P])

        consts_in = sem("consts_in")
        q_done = sem("q_done")
        q_ready = sem("q_ready")
        logits_ready = sem("logits_ready")
        mx_ready = sem("mx_ready")
        probs_ready = sem("probs_ready")
        turned = sem("turned")
        probsT_ready = sem("probsT_ready")
        pv_ready = sem("pv_ready")
        head_ready = sem("head_ready")
        out_done = sem("out_done")
        rinv_ready = sem("rinv_ready")
        x_added = sem("x_added")

        with nc.Block() as block:
            @block.sync
            def _(sp):
                sp.dma_start(wq[:, :, :], ins["Wq"]).then_inc(consts_in, 16)
                sp.dma_start(wo[:, :, :], ins["Wo"]).then_inc(consts_in, 16)
                sp.dma_start(ahead[:, :, :], ins["c_ahead"]).then_inc(consts_in, 16)

            @block.tensor
            def _(pe):
                pe.wait_ge(consts_in, 48)

                def logits_of(t, r, k, chunks):
                    u = H * t + k
                    for c in range(chunks):
                        diagonal = c == chunks - 1
                        nc.tensor.matmul(psL[:, c * CH:(c + 1) * CH], qT[:, k, :], keysT[:, k, c * CH:(c + 1) * CH],
                                         start=True, stop=not diagonal)
                    nc.tensor.matmul(psL[:, c * CH:(c + 1) * CH], big_ident[:, :], ahead[:, r, :],
                                     start=False, stop=True).then_inc(logits_ready, 1)

                def turn(k, q):
                    for s in range(4):
                        j = 4 * q + s
                        last = nc.tensor.transpose(psT[:, q % 2, s * P:(s + 1) * P],
                                                   probs[:, k % 2, j * P:(j + 1) * P], ident[:, :])
                    last.then_inc(turned, 1)

                def weigh(n, k, q, chunks):
                    pe.wait_ge(probsT_ready, n)
                    for s in range(4):
                        j = 4 * q + s
                        last = nc.tensor.matmul(psV[:, k % 2, :], values[:, j, k, :], probsT[:, j, :],
                                                start=(j == 0), stop=(j == 4 * chunks - 1))
                    if q == chunks - 1:
                        last.then_inc(pv_ready, 1)

                def project(t, k):
                    u = H * t + k
                    pe.wait_ge(head_ready, u + 1)
                    nc.tensor.matmul(psO[:, (k % 2) * P:(k % 2) * P + P], headT[:, k % 2, :], wo[:, k, :],
                                     start=True, stop=True).then_inc(out_done, 1)

                def tile(t, r, blocks_before, chunks):
                    for k in range(H):
                        nc.tensor.matmul(psT[:, k // 4, (k % 4) * P:(k % 4 + 1) * P], wq[:, k, :],
                                         xT[:, bass.ts(t, P)], start=True, stop=True).then_inc(q_done, 1)
                    pe.wait_ge(q_ready, 2 * t + 2)
                    logits_of(t, r, 0, chunks)
                    for k in range(H):
                        u = H * t + k
                        pe.wait_ge(probs_ready, u + 1)
                        if k < H - 1:
                            logits_of(t, r, k + 1, chunks)
                        n = blocks_before + k * chunks
                        turn(k, 0)
                        if k >= 1:
                            project(t, k - 1)
                        for q in range(chunks):
                            if q + 1 < chunks:
                                turn(k, q + 1)
                            weigh(n + q + 1, k, q, chunks)
                    project(t, H - 1)

                for g in range(NC):
                    with pe.Fori(0, TC) as r:
                        tile(r + g * TC, r, H * TC * (g * (g + 1) // 2) + r * (H * (g + 1)), g + 1)

            @block.scalar
            def _(act):
                def exp_of(t, k, chunks):
                    act.wait_ge(mx_ready, H * t + k + 1)
                    nc.scalar.activation(probs[:, k % 2, 0:chunks * CH], psL[:, 0:chunks * CH], ACT.Exp,
                                         bias=neg_mx[:, k % 2:k % 2 + 1],
                                         accum_out=rsum[:, k % 2:k % 2 + 1]).then_inc(probs_ready, 1)

                def tile(t, r, blocks_before, chunks):
                    for b in range(2):
                        act.wait_ge(q_done, H * t + 4 * b + 4)
                        nc.scalar.mul(qT[:, 4 * b:4 * b + 4, :].rearrange("p s c -> p (s c)"), psT[:, b, :],
                                      float(C) ** -0.5).then_inc(q_ready, 1)
                    exp_of(t, 0, chunks)
                    for k in range(H):
                        for q in range(chunks):
                            act.wait_ge(turned, blocks_before + k * chunks + q + 1)
                            nc.scalar.copy(probsT[:, 4 * q:4 * q + 4, :].rearrange("p s c -> p (s c)"),
                                           psT[:, q % 2, :]).then_inc(probsT_ready, 1)
                        if k < H - 1:
                            exp_of(t, k + 1, chunks)

                for g in range(NC):
                    with act.Fori(0, TC) as r:
                        tile(r + g * TC, r, H * TC * (g * (g + 1) // 2) + r * (H * (g + 1)), g + 1)

            @block.vector
            def _(dve):
                def max_of(t, k, chunks):
                    dve.wait_ge(logits_ready, H * t + k + 1)
                    nc.vector.tensor_reduce(neg_mx[:, k % 2:k % 2 + 1], psL[:, 0:chunks * CH],
                                            mybir.AxisListType.X, ALU.max, negate=True).then_inc(mx_ready, 1)

                def head_of(t, k):
                    dve.wait_ge(pv_ready, H * t + k + 1)
                    nc.vector.tensor_copy(headT[:, k % 2, :], psV[:, k % 2, :]).then_inc(head_ready, 1)
                    nc.vector.reciprocal(rinv[:, k % 2:k % 2 + 1], rsum[:, k % 2:k % 2 + 1]).then_inc(rinv_ready, 1)

                def add_head(t, k):
                    u = H * t + k
                    dve.wait_ge(rinv_ready, u + 1)
                    dve.wait_ge(out_done, u + 1)
                    nc.vector.scalar_tensor_tensor(X[:, t, :], psO[:, (k % 2) * P:(k % 2) * P + P],
                                                   rinv[:, k % 2:k % 2 + 1], X[:, t, :],
                                                   ALU.mult, ALU.add).then_inc(x_added, 1)

                def tile(t, chunks):
                    max_of(t, 0, chunks)
                    for k in range(H):
                        if k < H - 1:
                            max_of(t, k + 1, chunks)
                        if k >= 1:
                            add_head(t, k - 1)
                        head_of(t, k)
                    add_head(t, H - 1)

                for g in range(NC):
                    with dve.Fori(0, TC) as r:
                        tile(r + g * TC, g + 1)


def graph_attention(nc, ins, X, adj_neg, ident, big_ident, psL, psT, psV, psO):
    fp32 = mybir.dt.float32
    bf16 = mybir.dt.bfloat16
    ALU = mybir.AluOpType
    ACT = mybir.ActivationFunctionType
    SLOPE = 0.2
    with ExitStack() as ctx:
        def sb(name, shape, dt=fp32):
            return ctx.enter_context(nc.sbuf_tensor("ga_" + name, shape, dt))

        sem = stage_semaphores(nc, ctx, "ga_")

        vals = sb("vals", [P, T, H, C])
        w_out = sb("w_out", [P, H, C])
        b_out = sb("b_out", [P, C])
        s1_cols = sb("s1_cols", [P, T, H])
        s2_parts = sb("s2_parts", [3 * 32, N], bf16)
        s2_pick = sb("s2_pick", [3 * 32, H, P], bf16)
        relu_part = sb("relu_part", [P, N])
        logits = sb("logits", [P, N])
        probs = sb("probs", [P, N])
        probsT = sb("probsT", [P, T, P])
        mx = sb("mx", [P, 1])
        waited = sb("waited", [P, 1])
        neg_mx = sb("neg_mx", [P, 1])
        rsum = sb("rsum", [P, 1])
        rinv = sb("rinv", [P, 1])
        above = sb("above", [P, P])
        below = sb("below", [P, P])
        exp_below = sb("exp_below", [P, P])
        feat = sb("feat", [P, P])
        featT = sb("featT", [P, P])
        xT = logits
        w_all = relu_part[:, 0:H * C]
        w_heads_t = relu_part[:, H * C:2 * H * C].rearrange("d (h f) -> d h f", h=H)
        a_cols = probs[:, 0:2 * H]
        wa = probs[:, 64:64 + 2 * H]
        s2_rows = relu_part[0:H, :]
        s2_rest = probs[0:H, :]
        norm = Norm(nc, ctx, "ga_norm", X, xT[:, :], probsT, ident, psT)

        consts_in = sem("consts_in")
        wa_done = sem("wa_done")
        wa_copied = sem("wa_copied")
        vals_done = sem("vals_done")
        vals_copied = sem("vals_copied")
        s1_done = sem("s1_done")
        s2_done = sem("s2_done")
        s1_copied = sem("s1_copied")
        zeroed = sem("zeroed")
        split = sem("split")
        moved = sem("moved")
        logits_ready = sem("logits_ready")
        logits_seen = sem("logits_seen")
        relu_ready = sem("relu_ready")
        mx_found = sem("mx_found")
        mx_ready = sem("mx_ready")
        probs_ready = sem("probs_ready")
        turned = sem("turned")
        probsT_dve = sem("probsT_dve")
        probsT_act = sem("probsT_act")
        pv_ready = sem("pv_ready")
        rinv_ready = sem("rinv_ready")
        below_ready = sem("below_ready")
        exp_ready = sem("exp_ready")
        feat_ready = sem("feat_ready")
        feat_turned = sem("feat_turned")
        featT_ready = sem("featT_ready")
        projected = sem("projected")
        x_added = sem("x_added")

        with nc.Block() as block:
            @block.sync
            def _(sp):
                sp.dma_start(w_all, ins["W_all"]).then_inc(consts_in, 16)
                sp.dma_start(w_heads_t, ins["W_heads_t"]).then_inc(consts_in, 16)
                sp.dma_start(a_cols, ins["a_cols"]).then_inc(consts_in, 16)
                sp.dma_start(w_out[:, :, :], ins["W_out"]).then_inc(consts_in, 16)
                sp.dma_start(b_out[:, :], ins["b_out"].to_broadcast([P, C])).then_inc(consts_in, 16)
                sp.dma_start(s2_pick[:, :, :], ins["c_s2_pick"]).then_inc(consts_in, 16)

            @block.tensor
            def _(pe):
                norm.tensor(pe)
                pe.wait_ge(consts_in, 96)
                for a in range(2):
                    for k in range(H):
                        n = a * H + k
                        last = nc.tensor.matmul(psO[:, n:n + 1], w_heads_t[:, k, :], a_cols[:, n:n + 1],
                                                start=True, stop=True)
                last.then_inc(wa_done, 1)
                pe.wait_ge(norm.xT_done, T // 4)
                for t in range(T):
                    if t >= 2:
                        pe.wait_ge(vals_copied, t - 1)
                    for b in range(2):
                        last = nc.tensor.matmul(psL[:, (2 * (t % 2) + b) * CH:(2 * (t % 2) + b + 1) * CH],
                                                xT[:, t * P:(t + 1) * P], w_all[:, b * CH:(b + 1) * CH],
                                                start=True, stop=True)
                    last.then_inc(vals_done, 1)
                pe.wait_ge(wa_copied, 1)
                for t in range(T):
                    last = nc.tensor.matmul(psO[:, t * H:(t + 1) * H], xT[:, t * P:(t + 1) * P], wa[:, 0:H],
                                            start=True, stop=True)
                last.then_inc(s1_done, 1)
                pe.wait_ge(vals_copied, T)
                for c in range(NC):
                    last = nc.tensor.matmul(psL[0:H, c * CH:(c + 1) * CH], wa[:, H:2 * H],
                                            xT[:, c * CH:(c + 1) * CH], start=True, stop=True)
                last.then_inc(s2_done, 1)

                def logits_of(t, k, first=False):
                    for c in range(NC):
                        if c == 0 and not first:
                            pe.wait_ge(mx_ready, H * t + k)
                        nc.tensor.matmul(psL[:, c * CH:(c + 1) * CH], big_ident[:, :],
                                         adj_neg[:, t, c * CH:(c + 1) * CH], start=True, stop=False)
                        last = nc.tensor.matmul(psL[:, c * CH:(c + 1) * CH], s2_pick[:, k, :],
                                                s2_parts[:, c * CH:(c + 1) * CH], start=False, stop=True)
                    last.then_inc(logits_ready, 1)

                def turn(q):
                    for s in range(4):
                        j = 4 * q + s
                        last = nc.tensor.transpose(psT[:, q % 2, s * P:(s + 1) * P],
                                                   probs[:, j * P:(j + 1) * P], ident[:, :])
                    last.then_inc(turned, 1)

                def weigh(t, k, q):
                    u = H * t + k
                    if q < 2:
                        pe.wait_ge(probsT_dve, 2 * u + q + 1)
                    else:
                        pe.wait_ge(probsT_act, 2 * u + q - 1)
                    for s in range(4):
                        j = 4 * q + s
                        last = nc.tensor.matmul(psV[:, 0, :], probsT[:, j, :], vals[:, j, k, :],
                                                start=(j == 0), stop=(j == T - 1))
                    if q == 3:
                        last.then_inc(pv_ready, 1)

                def turn_feat(t, k):
                    pe.wait_ge(feat_ready, H * t + k + 1)
                    nc.tensor.transpose(psV[:, 1, :], feat[:, :], ident[:, :]).then_inc(feat_turned, 1)

                def project(t, k):
                    pe.wait_ge(featT_ready, H * t + k + 1)
                    last = nc.tensor.matmul(psO[:, 0:C], featT[:, :], w_out[:, k, :],
                                            start=(k == 0), stop=(k == H - 1))
                    if k == H - 1:
                        last.then_inc(projected, 1)

                def tile(t, last):
                    for k in range(H):
                        if k < H - 1:
                            logits_of(t, k + 1)
                        elif not last:
                            logits_of(t + 1, 0)
                        if k >= 1:
                            turn_feat(t, k - 1)
                        pe.wait_ge(probs_ready, H * t + k + 1)
                        turn(0)
                        turn(1)
                        if k >= 1:
                            project(t, k - 1)
                        weigh(t, k, 0)
                        turn(2)
                        weigh(t, k, 1)
                        turn(3)
                        weigh(t, k, 2)
                        weigh(t, k, 3)
                    turn_feat(t, H - 1)
                    project(t, H - 1)

                pe.wait_ge(split, 5)
                pe.wait_ge(s1_copied, 1)
                logits_of(0, 0, first=True)
                with pe.Fori(0, T - 1) as t:
                    tile(t, False)
                tile(T - 1, True)

            @block.scalar
            def _(act):
                norm.scalar(act)
                act.wait_ge(wa_done, 1)
                nc.scalar.copy(wa, psO[:, 0:2 * H]).then_inc(wa_copied, 1)
                for t in range(T):
                    act.wait_ge(vals_done, t + 1)
                    nc.scalar.copy(vals[:, t, :, :].rearrange("p h c -> p (h c)"),
                                   psL[:, (t % 2) * 2 * CH:(t % 2 + 1) * 2 * CH]).then_inc(vals_copied, 1)
                act.wait_ge(s1_done, 1)
                nc.scalar.mul(s1_cols[:, :, :].rearrange("p t h -> p (t h)"), psO[:, 0:T * H],
                              1.0 - SLOPE).then_inc(s1_copied, 1)
                act.wait_ge(s1_copied, 1)

                def relu_of(t, k):
                    act.wait_ge(logits_ready, H * t + k + 1)
                    act.sem_inc(logits_seen, 1)
                    nc.scalar.activation(relu_part[:, :], psL[:, :], ACT.Relu, bias=s1_cols[:, t, k:k + 1],
                                         scale=(1.0 - SLOPE) / SLOPE).then_inc(relu_ready, 1)

                def exp_of(t, k):
                    act.wait_ge(mx_ready, H * t + k + 1)
                    nc.scalar.activation(probs[:, :], logits[:, :], ACT.Exp, bias=neg_mx[:, :],
                                         accum_out=rsum[:, :]).then_inc(probs_ready, 1)

                def copy_turned(t, k, q):
                    act.wait_ge(turned, 4 * (H * t + k) + q + 1)
                    nc.scalar.copy(probsT[:, 4 * q:4 * q + 4, :].rearrange("p s c -> p (s c)"),
                                   psT[:, q % 2, :]).then_inc(probsT_act, 1)

                def exp_below_of(t, k):
                    act.wait_ge(below_ready, H * t + k + 1)
                    nc.scalar.activation(exp_below[:, :], below[:, :], ACT.Exp).then_inc(exp_ready, 1)

                def keep_featT(t, k):
                    act.wait_ge(feat_turned, H * t + k + 1)
                    nc.scalar.copy(featT[:, :], psV[:, 1, :]).then_inc(featT_ready, 1)

                def tile(t, last):
                    for k in range(H):
                        if k >= 1:
                            keep_featT(t, k - 1)
                        if k < H - 1 or not last:
                            relu_of(t + (k + 1) // H, (k + 1) % H)
                        copy_turned(t, k, 2)
                        copy_turned(t, k, 3)
                        if k < H - 1 or not last:
                            exp_of(t + (k + 1) // H, (k + 1) % H)
                        exp_below_of(t, k)
                    keep_featT(t, H - 1)

                act.wait_ge(split, 5)
                relu_of(0, 0)
                exp_of(0, 0)
                with act.Fori(0, T - 1) as t:
                    tile(t, False)
                tile(T - 1, True)

            @block.vector
            def _(dve):
                norm.vector(dve)
                nc.vector.memset(s2_parts[:, :], 0.0).then_inc(zeroed, 1)
                dve.wait_ge(zeroed, 1)
                dve.wait_ge(vals_copied, T)
                dve.wait_ge(s2_done, 1)
                dve.wait_ge(s1_done, 1)
                nc.vector.tensor_scalar(s2_rows, psL[0:H, :], SLOPE, None, ALU.mult).then_inc(split, 1)
                dve.wait_ge(split, 1)
                nc.vector.tensor_copy(s2_parts[0:H, :], s2_rows).then_inc(split, 1)
                dve.wait_ge(split, 2)
                nc.vector.tensor_tensor(s2_rest, s2_rows, s2_parts[0:H, :], ALU.subtract).then_inc(split, 1)
                dve.wait_ge(split, 3)
                nc.vector.tensor_copy(s2_parts[32:32 + H, :], s2_rest).then_inc(split, 1)
                dve.wait_ge(split, 4)
                nc.vector.tensor_copy(s2_rows, s2_parts[32:32 + H, :]).then_inc(moved, 1)
                dve.wait_ge(moved, 1)
                nc.vector.tensor_tensor(s2_parts[64:64 + H, :], s2_rest, s2_rows, ALU.subtract).then_inc(split, 1)

                def copy_turned(t, k, q):
                    dve.wait_ge(turned, 4 * (H * t + k) + q + 1)
                    nc.vector.tensor_copy(probsT[:, 4 * q:4 * q + 4, :].rearrange("p s c -> p (s c)"),
                                          psT[:, q % 2, :]).then_inc(probsT_dve, 1)

                def max_of(t, k):
                    u = H * t + k
                    dve.wait_ge(relu_ready, u + 1)
                    nc.vector.memset(waited[:, :], 0.0)
                    nc.vector.tensor_tensor_reduce(out=logits[:, :], in0=psL[:, :], in1=relu_part[:, :],
                                                   scale=1.0, scalar=-3.0e38, op0=ALU.add, op1=ALU.max,
                                                   accum_out=mx[:, :]).then_inc(mx_found, 1)
                    dve.wait_ge(mx_found, u + 1)
                    nc.vector.tensor_scalar(neg_mx[:, :], mx[:, :], -1.0, None, ALU.mult).then_inc(mx_ready, 1)

                def elu_of(t, k):
                    u = H * t + k
                    dve.wait_ge(rinv_ready, u + 1)
                    dve.wait_ge(pv_ready, u + 1)
                    nc.vector.tensor_scalar(above[:, :], psV[:, 0, :], rinv[:, :], 0.0, ALU.mult, ALU.max)
                    nc.vector.tensor_scalar(below[:, :], psV[:, 0, :], rinv[:, :], 0.0, ALU.mult, ALU.min
                                            ).then_inc(below_ready, 1)
                    dve.wait_ge(exp_ready, u + 1)
                    nc.vector.scalar_tensor_tensor(feat[:, :], exp_below[:, :], -1.0, above[:, :],
                                                   ALU.add, ALU.add).then_inc(feat_ready, 1)

                def sum_of(t, k):
                    dve.wait_ge(probs_ready, H * t + k + 1)
                    nc.vector.reciprocal(rinv[:, :], rsum[:, :]).then_inc(rinv_ready, 1)

                def tile(t, last):
                    for k in range(H):
                        sum_of(t, k)
                        copy_turned(t, k, 0)
                        copy_turned(t, k, 1)
                        if k < H - 1 or not last:
                            max_of(t + (k + 1) // H, (k + 1) % H)
                        elu_of(t, k)
                    dve.wait_ge(projected, t + 1)
                    nc.vector.tensor_tensor(X[:, t, :], X[:, t, :], psO[:, 0:C], ALU.add).then_inc(x_added, 1)
                    dve.wait_ge(x_added, 2 * t + 1)
                    nc.vector.tensor_tensor(X[:, t, :], X[:, t, :], b_out[:, :], ALU.add).then_inc(x_added, 1)

                max_of(0, 0)
                with dve.Fori(0, T - 1) as t:
                    tile(t, False)
                tile(T - 1, True)


def experts(nc, ins, X, ident, psL, psT, psO):
    fp32 = mybir.dt.float32
    u32 = mybir.dt.uint32
    ALU = mybir.AluOpType
    ACT = mybir.ActivationFunctionType
    E = 16
    F = 256
    FH = F // P
    TC = CH // P
    with ExitStack() as ctx:
        def sb(name, shape, dt=fp32):
            return ctx.enter_context(nc.sbuf_tensor("ex_" + name, shape, dt))

        sem = stage_semaphores(nc, ctx, "ex_")

        w1 = sb("w1", [P, E, F])
        b1 = sb("b1", [P, E, FH])
        w2 = sb("w2", [P, E, FH, C])
        b2 = sb("b2", [E, C])
        gate_w = sb("gate_w", [P, E])
        gate_b = sb("gate_b", [P, E])
        gamma = sb("gamma", [P, C])
        beta = sb("beta", [P, C])
        expert_no = sb("expert_no", [P, E])
        xT = sb("xT", [P, N])
        xn = sb("xn", [P, T, C])
        y = sb("y", [P, T, C])
        gates = sb("gates", [P, T, E])
        best = sb("best", [P, T, 8])
        best_at = sb("best_at", [P, T, 8], u32)
        gap = sb("gap", [P, T])
        second = sb("second", [P, T])
        both = sb("both", [P, T])
        share = sb("share", [P, 2, T])
        at_best = sb("at_best", [P, 2, T, E])
        wgt = sb("wgt", [P, T, E])
        wgtT = sb("wgtT", [E, N])
        hid = sb("hid", [P, 2, FH, CH])
        stats = sb("stats", [P, T, 6])
        mv = sb("mv", [P, T, 2])
        eps = sb("eps", [P, 1])
        std = sb("std", [P, T])
        norm = Norm(nc, ctx, "ex_norm", X, xT[:, :], xn, ident, psT)

        consts_in = sem("consts_in")
        gates_done = sem("gates_done")
        step = sem("step")
        gap_ready = sem("gap_ready")
        second_ready = sem("second_ready")
        wgt_ready = sem("wgt_ready")
        wgt_turned = sem("wgt_turned")
        wgtT_ready = sem("wgtT_ready")
        b2_done = sem("b2_done")
        b2_added = sem("b2_added")
        up_done = sem("up_done")
        hid_ready = sem("hid_ready")
        down_done = sem("down_done")
        bank_free = sem("bank_free")
        y_added = sem("y_added")
        moments = sem("moments")
        std_done = sem("std_done")
        finished = sem("finished")

        with nc.Block() as block:
            @block.sync
            def _(sp):
                sp.dma_start(w1[:, :, :], ins["w1"]).then_inc(consts_in, 16)
                sp.dma_start(w2[:, :, :, :], ins["w2"]).then_inc(consts_in, 16)
                sp.dma_start(b1[:, :, :], ins["b1"]).then_inc(consts_in, 16)
                sp.dma_start(b2[:, :], ins["b2"]).then_inc(consts_in, 16)
                sp.dma_start(gate_w[:, :], ins["gate_w"]).then_inc(consts_in, 16)
                sp.dma_start(gate_b[:, :], ins["gate_b"].to_broadcast([P, E])).then_inc(consts_in, 16)
                sp.dma_start(gamma[:, :], ins["gamma"].to_broadcast([P, C])).then_inc(consts_in, 16)
                sp.dma_start(beta[:, :], ins["beta"].to_broadcast([P, C])).then_inc(consts_in, 16)
                sp.dma_start(expert_no[:, :], ins["c_expert_no"]).then_inc(consts_in, 16)

            @block.tensor
            def _(pe):
                norm.tensor(pe)
                pe.wait_ge(consts_in, 144)
                pe.wait_ge(norm.xT_done, T // 4)
                for t in range(T):
                    last = nc.tensor.matmul(psO[:, t * E:(t + 1) * E], xT[:, t * P:(t + 1) * P], gate_w[:, :],
                                            start=True, stop=True)
                last.then_inc(gates_done, 1)
                pe.wait_ge(wgt_ready, 1)
                for t in range(T):
                    last = nc.tensor.transpose(psL[0:E, t * P:(t + 1) * P], wgt[:, t, :], ident[:, :])
                last.then_inc(wgt_turned, 1)
                pe.wait_ge(wgtT_ready, 1)
                for t in range(T):
                    last = nc.tensor.matmul(psL[:, t * P:(t + 1) * P], wgtT[:, t * P:(t + 1) * P], b2[:, :],
                                            start=True, stop=True)
                last.then_inc(b2_done, 1)
                pe.wait_ge(b2_added, 1)

                def up(c, e):
                    for f in range(FH):
                        b = FH * (e % 2) + f
                        last = nc.tensor.matmul(psL[:, b * CH:(b + 1) * CH], w1[:, e, f * P:(f + 1) * P],
                                                xT[:, bass.ts(c, CH)], start=True, stop=True)
                    last.then_inc(up_done, 1)

                def down(c, e):
                    v = E * c + e
                    pe.wait_ge(hid_ready, v + 1)
                    pe.wait_ge(bank_free, v + 1)
                    for s in range(TC):
                        for f in range(FH):
                            last = nc.tensor.matmul(psT[:, e % 2, s * P:(s + 1) * P],
                                                    hid[:, e % 2, f, s * P:(s + 1) * P], w2[:, e, f, :],
                                                    start=(f == 0), stop=(f == FH - 1))
                    last.then_inc(down_done, 1)

                with pe.Fori(0, NC) as c:
                    up(c, 0)
                    for e in range(E):
                        if e < E - 1:
                            up(c, e + 1)
                        down(c, e)

            @block.scalar
            def _(act):
                norm.scalar(act)
                act.wait_ge(gap_ready, 1)
                nc.scalar.activation(second[:, :], gap[:, :], ACT.Exp).then_inc(second_ready, 1)
                act.wait_ge(wgt_turned, 1)
                nc.scalar.copy(wgtT[:, :], psL[0:E, :]).then_inc(wgtT_ready, 1)
                with act.Fori(0, NC) as c:
                    for e in range(E):
                        act.wait_ge(up_done, E * c + e + 1)
                        for f in range(FH):
                            b = FH * (e % 2) + f
                            last = nc.scalar.activation(hid[:, e % 2, f, :], psL[:, b * CH:(b + 1) * CH], ACT.Relu,
                                                        bias=b1[:, e, f:f + 1])
                        last.then_inc(hid_ready, 1)
                act.wait_ge(moments, 1)
                nc.scalar.activation(std[:, :], mv[:, :, 1], ACT.Sqrt, bias=eps[:, :]).then_inc(std_done, 1)

            @block.vector
            def _(dve):
                norm.vector(dve)
                dve.sem_inc(bank_free, 2)
                dve.sem_inc(y_added, TC)
                c = Chain(dve, step)
                nc.vector.memset(eps[:, :], LN_EPS)
                dve.wait_ge(gates_done, 1)
                dve.wait_ge(consts_in, 144)
                a = c.did(nc.vector.tensor_tensor(gates[:, :, :], psO[:, 0:T * E].rearrange("p (t e) -> p t e", e=E),
                                                  gate_b[:, :].unsqueeze(1).to_broadcast([P, T, E]), ALU.add))
                dve.wait_ge(step, a)
                for t in range(T):
                    a = c.did(nc.vector.max(best[:, t, :], gates[:, t, :]))
                dve.wait_ge(step, a)
                for t in range(T):
                    a = c.did(nc.vector.max_index(best_at[:, t, :], best[:, t, :], gates[:, t, :]))
                nc.vector.tensor_tensor(gap[:, :], best[:, :, 1], best[:, :, 0], ALU.subtract).then_inc(gap_ready, 1)
                dve.wait_ge(second_ready, 1)
                a2 = c.did(nc.vector.tensor_scalar(both[:, :], second[:, :], 1.0, None, ALU.add))
                dve.wait_ge(step, a2)
                a3 = c.did(nc.vector.reciprocal(share[:, 0, :], both[:, :]))
                dve.wait_ge(step, a3)
                a4 = c.did(nc.vector.tensor_tensor(share[:, 1, :], share[:, 0, :], second[:, :], ALU.mult))
                dve.wait_ge(step, a4)
                for m in range(2):
                    b = c.did(nc.vector.tensor_tensor(at_best[:, m, :, :],
                                                      best_at[:, :, m:m + 1].to_broadcast([P, T, E]),
                                                      expert_no[:, :].unsqueeze(1).to_broadcast([P, T, E]),
                                                      ALU.is_equal))
                    dve.wait_ge(step, b)
                    b = c.did(nc.vector.tensor_tensor(at_best[:, m, :, :], at_best[:, m, :, :],
                                                      share[:, m, :].unsqueeze(2).to_broadcast([P, T, E]),
                                                      ALU.mult))
                dve.wait_ge(step, b)
                nc.vector.tensor_tensor(wgt[:, :, :], at_best[:, 0, :, :], at_best[:, 1, :, :],
                                        ALU.add).then_inc(wgt_ready, 1)
                dve.wait_ge(b2_done, 1)
                nc.vector.tensor_tensor(y[:, :, :].rearrange("p t c -> p (t c)"), psL[:, :],
                                        xn[:, :, :].rearrange("p t c -> p (t c)"), ALU.add).then_inc(b2_added, 1)
                dve.wait_ge(b2_added, 1)
                with dve.Fori(0, NC) as ch:
                    for e in range(E):
                        v = E * ch + e
                        dve.wait_ge(down_done, v + 1)
                        for s in range(TC):
                            t = TC * ch + s
                            dve.wait_ge(y_added, TC * v + s + 1)
                            last = nc.vector.scalar_tensor_tensor(
                                y[:, t, :], psT[:, e % 2, s * P:(s + 1) * P], wgt[:, t, e:e + 1], y[:, t, :],
                                ALU.mult, ALU.add)
                            last.then_inc(y_added, 1)
                        dve.wait_ge(y_added, TC * v + 2 * TC)
                        dve.sem_inc(bank_free, 1)
                for t in range(T):
                    last = c.did(nc.vector.bn_stats(stats[:, t, :], y[:, t, :]))
                dve.wait_ge(step, last)
                for t in range(T):
                    last = nc.vector.bn_aggr(mv[:, t, :], stats[:, t, :])
                last.then_inc(moments, 1)
                dve.wait_ge(std_done, 1)
                a = c.did(nc.vector.reciprocal(gap[:, :], std[:, :]))
                dve.wait_ge(step, a)
                for t in range(T):
                    a = c.did(nc.vector.tensor_scalar(y[:, t, :], y[:, t, :], mv[:, t, 0:1], gap[:, t:t + 1],
                                                      ALU.subtract, ALU.mult))
                dve.wait_ge(step, a)
                a = c.did(nc.vector.tensor_tensor(y[:, :, :], y[:, :, :],
                                                  gamma[:, :].unsqueeze(1).to_broadcast([P, T, C]), ALU.mult))
                dve.wait_ge(step, a)
                a = c.did(nc.vector.tensor_tensor(y[:, :, :], y[:, :, :],
                                                  beta[:, :].unsqueeze(1).to_broadcast([P, T, C]), ALU.add))
                dve.wait_ge(step, a)
                nc.vector.tensor_tensor(X[:, :, :], X[:, :, :], y[:, :, :], ALU.add).then_inc(finished, 1)
                dve.wait_ge(finished, 1)


def layouts(inputs):
    import numpy as np

    a = {k: np.asarray(v) for k, v in inputs.items()}
    rows = np.arange(P)
    node, head = rows // H, rows % H
    same_node = node[:, None] == np.arange(G)[None, :]
    bias_mask = np.full((KC + NF, P), -1.0, np.float32)
    bias_mask[:KC] = 2.0 * (np.arange(KC)[:, None] // NF == node[None, :])
    k_of = np.arange(P) // G
    i_of = np.arange(P) % G
    spread = (k_of[:, None, None] == np.arange(H)[None, :, None]) & (i_of[:, None, None] == node[None, None, :])
    s2_pick = np.zeros((3 * 32, H, P), np.float32)
    for m in range(3):
        s2_pick[32 * m + np.arange(H), np.arange(H), :] = 1.0
    return {
        "x": a["x"], "adj": a["adj"],
        "c_ident": np.eye(P, dtype=np.float32),
        "c_big_ident": (np.eye(P) * MASKED).astype(np.dtype("bfloat16")),
        "W_t": np.ascontiguousarray(a["L0_gnn_W"].T),
        "a_l": a["L0_gnn_a_l"].reshape(C, 1), "a_r": a["L0_gnn_a_r"].reshape(C, 1),
        "wc_tiled": np.tile(a["L0_gnn_Wc"].T, (G + 1, G)), "gate": a["L0_gnn_gate"].reshape(1, 1),
        "curv_t": np.ascontiguousarray(a["L0_gnn_curv_feats"].T),
        "curv_cols": np.ascontiguousarray(a["L0_gnn_curv_feats"].reshape(N // G, KC).T),
        "c_head_mask": ((rows[:, None] // D0) == head[None, :]).astype(np.float32),
        "c_bias_mask": bias_mask,
        "c_slope_rows": np.float32(0.2) * (np.arange(H)[:, None] == head[None, :]).astype(np.float32),
        "Wq_pk": np.ascontiguousarray(a["L0_ffn_Wq_pk"].reshape(C, 2, H, DK).transpose(0, 2, 1, 3)).reshape(C, H, P),
        "pk_keys": np.ascontiguousarray(a["L0_ffn_pk_keys"].transpose(0, 3, 2, 1)),
        "tables": np.concatenate([a["L0_ffn_keys_table"], a["L0_ffn_values_table"]], axis=1),
        "Wq": a["L0_ffn_Wq"].reshape(C, H, C),
        "Wo": np.ascontiguousarray(a["L0_ffn_Wo"].reshape(H, C, C).transpose(1, 0, 2)),
        "c_cand_no": np.tile(np.arange(CAND, dtype=np.float32), (P, 1)),
        "c_ahead": -(np.arange(CH)[None, None, :] > (P * np.arange(CH // P)[None, :, None] + rows[:, None, None])
                     ).astype(np.dtype("bfloat16")),
        "W_all": np.ascontiguousarray(a["L1_gnn_W_heads"].transpose(1, 0, 2)).reshape(C, H * C),
        "W_heads_t": np.ascontiguousarray(a["L1_gnn_W_heads"].transpose(2, 0, 1)),
        "a_cols": np.ascontiguousarray(np.concatenate([a["L1_gnn_a1"], a["L1_gnn_a2"]]).T),
        "W_out": np.ascontiguousarray(a["L1_gnn_W_out"].reshape(H, C, C).transpose(1, 0, 2)),
        "b_out": a["L1_gnn_b_out"].reshape(1, C),
        "w1": np.ascontiguousarray(a["L1_ffn_w1"].transpose(1, 0, 2)),
        "w2": np.ascontiguousarray(a["L1_ffn_w2"].reshape(16, 2, P, C).transpose(2, 0, 1, 3)),
        "b1": np.ascontiguousarray(a["L1_ffn_b1"].reshape(16, 2, P).transpose(2, 0, 1)),
        "b2": a["L1_ffn_b2"], "gate_w": a["L1_ffn_gate_w"], "gate_b": a["L1_ffn_gate_b"].reshape(1, 16),
        "gamma": a["L1_ffn_gamma"].reshape(1, C), "beta": a["L1_ffn_beta"].reshape(1, C),
        "c_expert_no": np.tile(np.arange(16, dtype=np.float32), (P, 1)),
        "c_s2_pick": s2_pick.astype(np.dtype("bfloat16")),
        "c_spread": (spread * MASKED).astype(np.dtype("bfloat16")),
        "c_fold": np.ascontiguousarray(spread.transpose(2, 1, 0)).astype(np.float32),
        "c_own_head": (head[:, None] == (rows[None, :] // D0)).astype(np.float32),
        "c_node_pick": same_node.astype(np.float32),
    }


def kernel(**inputs):
    import numpy as _np
    import concourse.bacc as _bacc
    from concourse import mybir as _mybir
    from concourse.bass_utils import run_bass_kernel_spmd as _run

    nc = _bacc.Bacc("TRN2", target_bir_lowering=False, num_devices=1)
    arrays, aps = {}, {}
    for name, a in layouts(inputs).items():
        arrays["in_" + name] = a
        aps[name] = nc.dram_tensor("in_" + name, a.shape, _mybir.dt.from_np(a.dtype), kind="ExternalInput").ap()
    out = nc.dram_tensor("out_0", (N, C), _mybir.dt.float32, kind="ExternalOutput").ap()
    program(nc, aps, out)
    r = _run(nc, [arrays], core_ids=[0])
    return r.results[0]["out_0"]
```

```python
import concourse.bass as bass
from concourse import mybir
from contextlib import ExitStack

N = 2048
C = 128
P = 128
T = N // P
H = 8
CH = 512
NC = N // CH
LN_EPS = 1e-5
MASKED = 2.0 ** 100

G = P // H
NF = 6
D0 = C // H
KC = G * NF


def program(nc, ins, out):
    fp32 = mybir.dt.float32
    bf16 = mybir.dt.bfloat16
    i32 = mybir.dt.int32
    ALU = mybir.AluOpType
    ACT = mybir.ActivationFunctionType
    X_AXIS = mybir.AxisListType.X

    with ExitStack() as whole:
        def keep(name, shape, dt):
            return whole.enter_context(nc.sbuf_tensor(name, shape, dt))

        X = keep("X", [P, T, C], fp32)
        ident = keep("ident", [P, P], fp32)
        big_ident = keep("big_ident", [P, P], bf16)
        psL = whole.enter_context(nc.psum_tensor("psL", [P, N], fp32))
        psT = whole.enter_context(nc.psum_tensor("psT", [P, 2, CH], fp32))
        psV = whole.enter_context(nc.psum_tensor("psV", [P, 4, P], fp32))
        psO = whole.enter_context(nc.psum_tensor("psO", [P, CH], fp32))

        load_rows(nc, ins, X, ident, big_ident)
        keysT_dram = nc.dram_tensor("keysT_scratch", (T, P, H, C), fp32).ap()
        values_dram = nc.dram_tensor("values_scratch", (T, P, H, C), fp32).ap()
        curvature_and_keys(nc, ins, X, ident, psL, psT, psV, psO, keysT_dram, values_dram)
        causal_attention(nc, ins, X, keysT_dram, values_dram, ident, big_ident, psL, psT, psV, psO)
        with nc.sbuf_tensor("adj_neg1", [P, T, N], bf16) as adj_neg:
            load_adjacency(nc, ins, "a1", adj_neg)
            graph_attention(nc, ins, X, adj_neg, ident, big_ident, psL, psT, psV, psO)
        experts(nc, ins, X, ident, psL, psT, psO)
        store_stage(nc, X, out)


def load_rows(nc, ins, X, ident, big_ident):
    with ExitStack() as ctx:
        rows_loaded = ctx.enter_context(nc.semaphore("rows_loaded"))
        with nc.Block() as block:
            @block.sync
            def _(sp):
                sp.dma_start(X[:, :, :], ins["x"].rearrange("(t p) c -> p t c", p=P)).then_inc(rows_loaded, 16)
                sp.dma_start(ident[:, :], ins["c_ident"]).then_inc(rows_loaded, 16)
                sp.dma_start(big_ident[:, :], ins["c_big_ident"]).then_inc(rows_loaded, 16)
                sp.wait_ge(rows_loaded, 48)


def load_adjacency(nc, ins, name, adj_neg):
    ALU = mybir.AluOpType
    SLOTS = 4
    with ExitStack() as ctx:
        raw = ctx.enter_context(nc.sbuf_tensor(name + "_adj_raw", [P, SLOTS, N], mybir.dt.int32))
        adj_loaded = [ctx.enter_context(nc.semaphore(f"{name}_adj_loaded{s}")) for s in range(SLOTS)]
        adj_turned = ctx.enter_context(nc.semaphore(name + "_adj_turned"))
        adj_v = ins["adj"].rearrange("(t p) j -> p t j", p=P)
        with nc.Block() as block:
            @block.sync
            def _(sp):
                for t in range(T):
                    if t >= SLOTS:
                        sp.wait_ge(adj_turned, t - SLOTS + 1)
                    sp.dma_start(raw[:, t % SLOTS, :], adj_v[:, t, :]).then_inc(adj_loaded[t % SLOTS], 16)

            @block.vector
            def _(dve):
                for t in range(T):
                    dve.wait_ge(adj_loaded[t % SLOTS], 16 * (t // SLOTS + 1))
                    nc.vector.tensor_scalar(adj_neg[:, t, :], raw[:, t % SLOTS, :], 0.0, -1.0,
                                            ALU.is_gt, ALU.add).then_inc(adj_turned, 1)


def store_stage(nc, X, out):
    with ExitStack() as ctx:
        stored = ctx.enter_context(nc.semaphore("stored"))
        with nc.Block() as block:
            @block.sync
            def _(sp):
                sp.dma_start(out.rearrange("(t p) c -> p t c", p=P), X[:, :, :]).then_inc(stored, 16)
                sp.wait_ge(stored, 16)


def stage_semaphores(nc, ctx, prefix):
    taken = []

    def give_back():
        nc.clear_and_free_semaphores(taken)
        nc.all_engine_barrier()

    ctx.callback(give_back)

    def sem(name):
        taken.append(nc.alloc_semaphore(prefix + name))
        return taken[-1]

    return sem


class Norm:

    def __init__(self, nc, ctx, name, X, xT, xn, ident, psT):
        def sb(what, shape):
            return ctx.enter_context(nc.sbuf_tensor(f"{name}_{what}", shape, mybir.dt.float32))

        def sem(what):
            return ctx.enter_context(nc.semaphore(f"{name}_{what}"))

        self.nc, self.X, self.xT, self.ident, self.psT = nc, X, xT, ident, psT
        self.stats = sb("stats", [P, T, 6])
        self.mv = sb("mv", [P, T, 2])
        self.eps = sb("eps", [P, 1])
        self.std = sb("std", [P, T])
        self.rstd = sb("rstd", [P, T])
        self.xn = xn
        self.stats_done = sem("stats_done")
        self.moments = sem("moments")
        self.std_done = sem("std_done")
        self.rstd_done = sem("rstd_done")
        self.xn_done = sem("xn_done")
        self.turned = sem("turned")
        self.xT_done = sem("xT_done")

    def vector(self, dve):
        nc = self.nc
        nc.vector.memset(self.eps[:, :], LN_EPS)
        for t in range(T):
            last = nc.vector.bn_stats(self.stats[:, t, :], self.X[:, t, :])
        last.then_inc(self.stats_done, 1)
        dve.wait_ge(self.stats_done, 1)
        for t in range(T):
            last = nc.vector.bn_aggr(self.mv[:, t, :], self.stats[:, t, :])
        last.then_inc(self.moments, 1)
        dve.wait_ge(self.std_done, 1)
        nc.vector.reciprocal(self.rstd[:, :], self.std[:, :]).then_inc(self.rstd_done, 1)
        dve.wait_ge(self.rstd_done, 1)
        for t in range(T):
            nc.vector.tensor_scalar(self.xn[:, t, :], self.X[:, t, :], self.mv[:, t, 0:1], self.rstd[:, t:t + 1],
                                    mybir.AluOpType.subtract, mybir.AluOpType.mult).then_inc(self.xn_done, 1)

    def scalar(self, act):
        nc = self.nc
        act.wait_ge(self.moments, 1)
        nc.scalar.activation(self.std[:, :], self.mv[:, :, 1], mybir.ActivationFunctionType.Sqrt,
                             bias=self.eps[:, :]).then_inc(self.std_done, 1)
        for q in range(T // 4):
            act.wait_ge(self.turned, q + 1)
            nc.scalar.copy(self.xT[:, 4 * q * P:4 * (q + 1) * P], self.psT[:, q % 2, :]).then_inc(self.xT_done, 1)

    def tensor(self, pe):
        nc = self.nc
        for t in range(T):
            q = t // 4
            if t % 4 == 0 and q >= 2:
                pe.wait_ge(self.xT_done, q - 1)
            pe.wait_ge(self.xn_done, t + 1)
            last = nc.tensor.transpose(self.psT[:, q % 2, (t % 4) * P:(t % 4 + 1) * P], self.xn[:, t, :],
                                       self.ident[:, :])
            if t % 4 == 3:
                last.then_inc(self.turned, 1)


class Chain:

    def __init__(self, engine, semaphore):
        self.engine, self.semaphore, self.count = engine, semaphore, 0

    def did(self, instruction):
        instruction.then_inc(self.semaphore, 1)
        self.count += 1
        return self.count

    def restart(self):
        self.engine.wait_ge(self.semaphore, self.count)
        self.engine.sem_clear(self.semaphore)
        self.count = 0


NK = 128
DK = C // 2
TOP = 16
RUNS = [(0, 1, 16), (1, 1, 8), (2, 1, 5), (3, 1, 4), (4, 1, 3), (5, 3, 2), (8, 8, 1)]
CAND = sum(rows * cols for _, rows, cols in RUNS)
RING = 2 * TOP


def curvature_and_keys(nc, ins, X, ident, psL, psT, psV, psO, keysT_out, values_out):
    fp32 = mybir.dt.float32
    bf16 = mybir.dt.bfloat16
    u32 = mybir.dt.uint32
    ALU = mybir.AluOpType
    ACT = mybir.ActivationFunctionType
    SLOPE = 0.2
    UNITS = N // G
    KU = UNITS // T
    KW = KC + NF
    KB = KW + H
    LOWEST = -3.0e38
    assert KU == H
    with ExitStack() as ctx:
        def sb(name, shape, dt=fp32):
            return ctx.enter_context(nc.sbuf_tensor("ck_" + name, shape, dt))

        sem = stage_semaphores(nc, ctx, "ck_")

        adj_raw = sb("adj_raw", [P, N], mybir.dt.int32)
        adj_neg = sb("adj_neg", [P, N], bf16)
        vals = sb("vals", [P, T, C])
        er_rows = sb("er_rows", [P, N])
        el_cols = sb("el_cols", [P, UNITS])
        c_cols = sb("c_cols", [KC, UNITS])
        c_rows = sb("c_rows", [KC, N])
        bias_rhs = sb("bias_rhs", [KB, 2, N])
        bias_w = sb("bias_w", [KB, P])
        spread = sb("spread", [P, KU, P], bf16)
        fold = sb("fold", [P, KU, P])
        own_head = sb("own_head", [P, P])
        node_pick = sb("node_pick", [P, G])
        relu_part = sb("relu_part", [P, N])
        logits = sb("logits", [P, N])
        probs = sb("probs", [P, N])
        probsT = sb("probsT", [P, T, P])
        mx = sb("mx", [P, 1])
        waited = sb("waited", [P, 1])
        neg_mx = sb("neg_mx", [P, 1])
        rsum = sb("rsum", [P, 2])
        rinv = sb("rinv", [P, 2])
        picked = sb("picked", [P, 2, P])
        xT = logits[:, :]
        hT = relu_part[:, :]
        el_wide = probs[:, :]
        norm = Norm(nc, ctx, "ck_norm", X, xT, probsT, ident, psT)

        wq = sb("wq", [P, H, P])
        keys = sb("keys", [P, H, 2 * NK])
        cand_no = sb("cand_no", [P, CAND])
        row_stats = sb("row_stats", [P, 6])
        row_mv = sb("row_mv", [P, 2])
        eps = sb("eps", [P, 1])
        row_std = sb("row_std", [P, 1])
        row_rstd = sb("row_rstd", [P, 1])
        row_xn = sb("row_xn", [P, C])
        row_xT = sb("row_xT", [C, P])
        qT = sb("qT", [P, P])
        sim = sb("sim", [P, 2, 2, NK])
        rest = sb("rest", [P, 2, NK])
        best = sb("best", [P, 2, TOP])
        best_at = sb("best_at", [P, 2, TOP], u32)
        at0 = sb("at0", [P, TOP])
        at1 = sb("at1", [P, TOP])
        cand = sb("cand", [P, CAND])
        cand_rest = sb("cand_rest", [P, CAND])
        cand_row = sb("cand_row", [P, CAND])
        top = sb("top", [P, TOP])
        top_at = sb("top_at", [P, TOP], u32)
        hit = sb("hit", [P, TOP, CAND])
        neg_top = sb("neg_top", [P, 1])
        raw_w = sb("raw_w", [P, H, TOP])
        sum_w = sb("sum_w", [P, H])
        inv_w = sb("inv_w", [P, H])
        rows = sb("rows", [P, H, TOP], u32)
        ring = sb("ring", [P, RING, 2 * C])
        part = sb("part", [P, 2, 2 * C])
        total = sb("total", [P, C])
        keys_tile = sb("keys_tile", [P, H, C])
        values_tile = sb("values_tile", [P, H, C])
        w_t = ring[:, 0, 0:P]
        al_w = ring[:, 0, P:2 * P]
        ar_w = ring[:, 1, 0:P]
        head_mask = ring[:, 1, P:2 * P]
        wc_raw = ring[0:KW, 2, 0:P]
        bias_mask = ring[0:KW, 2, P:2 * P]
        al_col = ring[:, 3, 0:1]
        ar_col = ring[:, 3, 1:2]
        gate_col = ring[0:KW, 3, 2:3]

        consts_in = sem("consts_in")
        mats_in = sem("mats_in")
        keys_in = sem("keys_in")
        keys_zeroed = sem("keys_zeroed")
        weights_ready = sem("weights_ready")
        prep_mm = sem("prep_mm")
        prep_copied = sem("prep_copied")
        er8_in = sem("er8_in")
        cols_ready = sem("cols_ready")
        el_mult = sem("el_mult")
        bias_ready = sem("bias_ready")
        adj_loaded = sem("adj_loaded")
        adj_turned = sem("adj_turned")
        diff_ready = sem("diff_ready")
        relu_ready = sem("relu_ready")
        logits_ready = sem("logits_ready")
        mx_found = sem("mx_found")
        mx_ready = sem("mx_ready")
        probs_ready = sem("probs_ready")
        turned = sem("turned")
        probsT_ready = sem("probsT_ready")
        pv_ready = sem("pv_ready")
        rinv_ready = sem("rinv_ready")
        picked_ready = sem("picked_ready")
        folded = sem("folded")
        x_added = sem("x_added")
        stats_ready = sem("stats_ready")
        moments_ready = sem("moments_ready")
        std_ready = sem("std_ready")
        rstd_ready = sem("rstd_ready")
        xn_ready = sem("xn_ready")
        xn_turned = sem("xn_turned")
        xT_ready = sem("xT_ready")
        qT_done = sem("qT_done")
        qT_copied = sem("qT_copied")
        sim_done = sem("sim_done")
        sim_copied = sem("sim_copied")
        sim_seen = sem("sim_seen")
        sim_free = sem("sim_free")
        top_ready = sem("top_ready")
        exp_ready = sem("exp_ready")
        rows_ready = sem("rows_ready")
        rows_seen = sem("rows_seen")
        ring_free = sem("ring_free")
        ring_seen = sem("ring_seen")
        got = [sem(f"got{i}") for i in range(RING)]
        step = sem("step")
        total_ready = sem("total_ready")
        key_turned = sem("key_turned")
        key_copied = sem("key_copied")
        keys_stored = sem("keys_stored")
        values_stored = sem("values_stored")
        keys_tile_free = sem("keys_tile_free")
        values_tile_free = sem("values_tile_free")

        def each_tile(engine, tile):
            tile(0, s1=True, last=False, choosing=False, adding=False)
            tile(1, s1=True, last=False, choosing=True, adding=False)
            with engine.Fori(2, T - 1) as t:
                tile(t, s1=True, last=False, choosing=True, adding=True)
            tile(T - 1, s1=True, last=True, choosing=True, adding=True)
            tile(T, s1=False, last=True, choosing=True, adding=True)
            tile(T + 1, s1=False, last=True, choosing=False, adding=True)

        with nc.Block() as block:
            @block.sync
            def _(sp):
                adj_v = ins["adj"].rearrange("(t p) j -> p t j", p=P)
                with nc.allow_non_contiguous_dma(reason="columns of one value"):
                    sp.dma_start(w_t, ins["W_t"]).then_inc(mats_in, 16)
                    sp.dma_start(al_col, ins["a_l"]).then_inc(mats_in, 16)
                    sp.dma_start(ar_col, ins["a_r"]).then_inc(mats_in, 16)
                    sp.dma_start(head_mask, ins["c_head_mask"]).then_inc(mats_in, 16)
                    sp.dma_start(bias_mask, ins["c_bias_mask"]).then_inc(mats_in, 16)
                    sp.dma_start(wc_raw, ins["wc_tiled"]).then_inc(mats_in, 16)
                    sp.dma_start(gate_col, ins["gate"].to_broadcast([KW, 1])).then_inc(mats_in, 16)
                sp.dma_start(adj_raw[:, :], adj_v[:, 0, :]).then_inc(adj_loaded, 16)
                for i in range(G):
                    sp.dma_start(c_rows[i * NF:(i + 1) * NF, :], ins["curv_t"]).then_inc(consts_in, 16)
                sp.dma_start(bias_w[KW:KB, :], ins["c_slope_rows"]).then_inc(consts_in, 16)
                for b in range(2):
                    sp.dma_start(bias_rhs[KC:KW, b, :], ins["curv_t"]).then_inc(consts_in, 16)
                sp.dma_start(c_cols[:, :], ins["curv_cols"]).then_inc(consts_in, 16)
                sp.dma_start(spread[:, :, :], ins["c_spread"]).then_inc(consts_in, 16)
                sp.dma_start(fold[:, :, :], ins["c_fold"]).then_inc(consts_in, 16)
                sp.dma_start(own_head[:, :], ins["c_own_head"]).then_inc(consts_in, 16)
                sp.dma_start(node_pick[:, :], ins["c_node_pick"]).then_inc(consts_in, 16)
                sp.wait_ge(prep_copied, 13)
                for b in range(2):
                    sp.dma_start(bias_rhs[KW:KB, b, :], er_rows[0:H, :]).then_inc(er8_in, 16)
                sp.dma_start(wq[:, :, :], ins["Wq_pk"]).then_inc(keys_in, 16)
                sp.dma_start(cand_no[:, :], ins["c_cand_no"]).then_inc(keys_in, 16)
                sp.wait_ge(keys_zeroed, 1)
                for p in range(2):
                    sp.dma_start(keys[p * DK:(p + 1) * DK, :, p * NK:(p + 1) * NK],
                                 ins["pk_keys"][p, :, :, :]).then_inc(keys_in, 16)

                def tile(t, s1, last, choosing, adding):
                    if not last:
                        sp.wait_ge(adj_turned, t + 1)
                        sp.dma_start(adj_raw[:, :], adj_v[:, t + 1, :]).then_inc(adj_loaded, 16)
                    if adding:
                        sp.wait_ge(key_copied, H * (t - 1))
                        sp.dma_start(keysT_out[t - 2, :, :, :], keys_tile[:, :, :]).then_inc(keys_stored, 16)
                        sp.wait_ge(total_ready, H * (t - 1))
                        sp.dma_start(values_out[t - 2, :, :, :], values_tile[:, :, :]).then_inc(values_stored, 16)
                        sp.wait_ge(keys_stored, 16 * (t - 1))
                        sp.sem_inc(keys_tile_free, 1)
                        sp.wait_ge(values_stored, 16 * (t - 1))
                        sp.sem_inc(values_tile_free, 1)

                sp.sem_inc(keys_tile_free, 1)
                sp.sem_inc(values_tile_free, 1)
                each_tile(sp, tile)

            @block.gpsimd
            def _(pool):
                with pool.Fori(0, T) as t:
                    for k in range(H):
                        u = H * t + k
                        pool.wait_ge(rows_ready, u + 1)
                        pool.sem_inc(rows_seen, 1)
                        pool.wait_ge(ring_free, u + 1)
                        pool.sem_inc(ring_seen, 1)
                        for s in range(TOP):
                            slot = (k % 2) * TOP + s
                            pool.indirect_dma_start(ring[:, slot, :], None, ins["tables"],
                                                    bass.IndirectOffsetOnAxis(rows[:, k, s:s + 1], axis=0)
                                                    ).then_inc(got[slot], 16)

            @block.tensor
            def _(pe):
                norm.tensor(pe)
                pe.wait_ge(norm.xT_done, T // 4)
                pe.wait_ge(mats_in, 16 * 7)
                for c in range(NC):
                    nc.tensor.matmul(psL[:, c * CH:(c + 1) * CH], w_t, xT[:, c * CH:(c + 1) * CH],
                                     start=True, stop=True).then_inc(prep_mm, 1)
                for q in range(4):
                    pe.wait_ge(prep_copied, 4 + q)
                    for s in range(4):
                        j = 4 * q + s
                        last = nc.tensor.matmul(psT[:, q % 2, s * P:(s + 1) * P], xT[:, j * P:(j + 1) * P], w_t,
                                                start=True, stop=True)
                    last.then_inc(prep_mm, 1)
                pe.wait_ge(weights_ready, 2)
                pe.wait_ge(prep_copied, 8)
                for c in range(NC):
                    nc.tensor.matmul(psL[:, c * CH:(c + 1) * CH], al_w, hT[:, c * CH:(c + 1) * CH],
                                     start=True, stop=True).then_inc(prep_mm, 1)
                for c in range(NC):
                    pe.wait_ge(prep_copied, 9 + c)
                    nc.tensor.matmul(psL[:, c * CH:(c + 1) * CH], ar_w, hT[:, c * CH:(c + 1) * CH],
                                     start=True, stop=True).then_inc(prep_mm, 1)

                def logits_of(t, k, first=False):
                    u = KU * t + k
                    if not first:
                        pe.wait_ge(mx_ready, u)
                    if k == 0:
                        pe.wait_ge(adj_turned, t + 1)
                    for c in range(NC):
                        nc.tensor.matmul(psL[:, c * CH:(c + 1) * CH], spread[:, k, :],
                                         adj_neg[:, c * CH:(c + 1) * CH], start=True, stop=False)
                        if c == 0:
                            pe.wait_ge(diff_ready, u + 1)
                        last = nc.tensor.matmul(psL[:, c * CH:(c + 1) * CH], bias_w[:, :],
                                                bias_rhs[:, k % 2, c * CH:(c + 1) * CH], start=False, stop=True)
                    last.then_inc(logits_ready, 1)

                def turn(q):
                    for s in range(4):
                        j = 4 * q + s
                        last = nc.tensor.transpose(psT[:, q % 2, s * P:(s + 1) * P],
                                                   probs[:, j * P:(j + 1) * P], ident[:, :])
                    last.then_inc(turned, 1)

                def weigh(t, k, q):
                    pe.wait_ge(probsT_ready, 4 * (KU * t + k) + q + 1)
                    for s in range(4):
                        j = 4 * q + s
                        last = nc.tensor.matmul(psV[:, k % 2, :], probsT[:, j, :], vals[:, j, :],
                                                start=(j == 0), stop=(j == T - 1))
                    if q == 3:
                        last.then_inc(pv_ready, 1)

                def fold_in(t, k):
                    pe.wait_ge(picked_ready, KU * t + k + 1)
                    last = nc.tensor.matmul(psO[:, 0:P], fold[:, k, :], picked[:, k % 2, :],
                                            start=(k == 0), stop=(k == KU - 1))
                    if k == KU - 1:
                        last.then_inc(folded, 1)

                def tile(t, s1, last, choosing, adding):
                    for k in range(H):
                        v = H * (t - 1) + k
                        u = H * (t - 2) + k
                        if choosing:
                            if k == 0:
                                pe.wait_ge(xT_ready, t)
                            elif adding:
                                pe.wait_ge(key_copied, u)
                            nc.tensor.matmul(psT[:, 0, 0:P], wq[:, k, :], row_xT[:, :],
                                             start=True, stop=True).then_inc(qT_done, 1)
                        if s1:
                            if k < KU - 1:
                                logits_of(t, k + 1)
                            elif not last:
                                logits_of(t + 1, 0)
                            if k >= 1:
                                fold_in(t, k - 1)
                        if choosing:
                            pe.wait_ge(qT_copied, v + 1)
                            nc.tensor.matmul(psT[:, 1, 0:2 * NK], qT[:, :], keys[:, k, :],
                                             start=True, stop=True).then_inc(sim_done, 1)
                        if s1:
                            pe.wait_ge(probs_ready, KU * t + k + 1)
                            turn(0)
                            if choosing:
                                pe.wait_ge(sim_copied, v + 1)
                            turn(1)
                            weigh(t, k, 0)
                            turn(2)
                            weigh(t, k, 1)
                            turn(3)
                            weigh(t, k, 2)
                            weigh(t, k, 3)
                        elif choosing:
                            pe.wait_ge(sim_copied, v + 1)
                        if adding:
                            if not choosing:
                                pe.wait_ge(key_copied, u)
                            pe.wait_ge(total_ready, u + 1)
                            nc.tensor.transpose(psT[:, 0, 0:P], total[:, :], ident[:, :]).then_inc(key_turned, 1)
                    if s1:
                        fold_in(t, KU - 1)
                        if adding:
                            pe.wait_ge(key_copied, H * (t - 1))
                        pe.wait_ge(xn_ready, t + 1)
                        nc.tensor.transpose(psT[:, 0, 0:P], row_xn[:, :], ident[:, :]).then_inc(xn_turned, 1)

                pe.wait_ge(consts_in, 16 * (G + 8))
                pe.wait_ge(bias_ready, 1)
                pe.wait_ge(er8_in, 32)
                pe.wait_ge(prep_copied, 16)
                pe.wait_ge(keys_in, 64)
                logits_of(0, 0, first=True)
                each_tile(pe, tile)

            @block.scalar
            def _(act):
                norm.scalar(act)
                for c in range(NC):
                    act.wait_ge(prep_mm, c + 1)
                    nc.scalar.copy(hT[:, c * CH:(c + 1) * CH], psL[:, c * CH:(c + 1) * CH]).then_inc(prep_copied, 1)
                for q in range(4):
                    act.wait_ge(prep_mm, 4 + q + 1)
                    nc.scalar.copy(vals[:, 4 * q:4 * q + 4, :].rearrange("p s c -> p (s c)"),
                                   psT[:, q % 2, :]).then_inc(prep_copied, 1)
                for c in range(NC):
                    act.wait_ge(prep_mm, 8 + c + 1)
                    nc.scalar.mul(el_wide[:, c * CH:(c + 1) * CH], psL[:, c * CH:(c + 1) * CH],
                                  1.0 - SLOPE).then_inc(prep_copied, 1)
                act.wait_ge(prep_mm, 16)
                nc.scalar.copy(er_rows[:, :], psL[:, :]).then_inc(prep_copied, 4)
                act.wait_ge(cols_ready, 1)
                act.wait_ge(prep_copied, 16)

                def relu_of(t, k):
                    u = KU * t + k
                    nc.scalar.activation(relu_part[:, :], er_rows[:, :], ACT.Relu,
                                         bias=el_cols[:, bass.ds(u, 1)], scale=1.0 - SLOPE).then_inc(relu_ready, 1)

                def exp_of(t, k):
                    act.wait_ge(mx_ready, KU * t + k + 1)
                    nc.scalar.activation(probs[:, :], logits[:, :], ACT.Exp, bias=neg_mx[:, :],
                                         accum_out=rsum[:, k % 2:k % 2 + 1]).then_inc(probs_ready, 1)

                def copy_turned(t, k):
                    for q in range(4):
                        act.wait_ge(turned, 4 * (KU * t + k) + q + 1)
                        nc.scalar.copy(probsT[:, 4 * q:4 * q + 4, :].rearrange("p s c -> p (s c)"),
                                       psT[:, q % 2, :]).then_inc(probsT_ready, 1)

                def tile(t, s1, last, choosing, adding):
                    for k in range(H):
                        v = H * (t - 1) + k
                        ahead = k < KU - 1 or not last
                        if choosing:
                            act.wait_ge(qT_done, v + 1)
                            nc.scalar.copy(qT[:, :], psT[:, 0, 0:P]).then_inc(qT_copied, 1)
                        if s1 and ahead:
                            relu_of(t, k + 1)
                        if choosing:
                            act.wait_ge(sim_done, v + 1)
                            act.wait_ge(sim_free, v + 1)
                            nc.scalar.copy(sim[:, k % 2, :, :].rearrange("p a b -> p (a b)"),
                                           psT[:, 1, 0:2 * NK]).then_inc(sim_copied, 1)
                        if s1:
                            copy_turned(t, k)
                            if ahead:
                                exp_of(t + (k + 1) // KU, (k + 1) % KU)
                        if adding:
                            if k == 0:
                                act.wait_ge(keys_tile_free, t - 1)
                            act.wait_ge(key_turned, H * (t - 2) + k + 1)
                            nc.scalar.copy(keys_tile[:, k, :], psT[:, 0, 0:P]).then_inc(key_copied, 1)
                        if choosing:
                            act.wait_ge(top_ready, v + 1)
                            nc.scalar.activation(raw_w[:, k, :], top[:, :], ACT.Exp, bias=neg_top[:, :],
                                                 accum_out=sum_w[:, k:k + 1]).then_inc(exp_ready, 1)
                    if s1:
                        act.wait_ge(moments_ready, t + 1)
                        nc.scalar.activation(row_std[:, :], row_mv[:, 1:2], ACT.Sqrt, bias=eps[:, :]
                                             ).then_inc(std_ready, 1)
                        act.wait_ge(xn_turned, t + 1)
                        nc.scalar.copy(row_xT[:, :], psT[:, 0, 0:P]).then_inc(xT_ready, 1)

                relu_of(0, 0)
                exp_of(0, 0)
                each_tile(act, tile)

            @block.vector
            def _(dve):
                norm.vector(dve)
                nc.vector.memset(keys[:, :, :], 0.0).then_inc(keys_zeroed, 1)
                nc.vector.memset(eps[:, :], LN_EPS)
                dve.sem_inc(sim_free, 2)
                dve.sem_inc(ring_free, 2)
                dve.wait_ge(mats_in, 16 * 7)
                nc.vector.tensor_scalar(al_w, head_mask, al_col, None, ALU.mult).then_inc(weights_ready, 1)
                nc.vector.tensor_scalar(ar_w, head_mask, ar_col, None, ALU.mult).then_inc(weights_ready, 1)
                nc.vector.scalar_tensor_tensor(bias_w[0:KW, :], wc_raw, gate_col, bias_mask,
                                               ALU.mult, ALU.mult).then_inc(bias_ready, 1)
                dve.wait_ge(consts_in, 16 * (G + 8))
                dve.wait_ge(prep_copied, 12)
                nc.vector.tensor_tensor(el_wide.rearrange("p (u i) -> p u i", i=G),
                                        el_wide.rearrange("p (u i) -> p u i", i=G),
                                        node_pick[:, :].unsqueeze(1).to_broadcast([P, UNITS, G]),
                                        ALU.mult).then_inc(el_mult, 1)
                dve.wait_ge(el_mult, 1)
                nc.vector.tensor_reduce(el_cols[:, :], el_wide.rearrange("p (u i) -> p u i", i=G),
                                        mybir.AxisListType.X, ALU.add).then_inc(cols_ready, 1)
                c = Chain(dve, step)

                def turn_adj(t):
                    dve.wait_ge(adj_loaded, 16 * (t + 1))
                    nc.vector.tensor_scalar(adj_neg[:, :], adj_raw[:, :], 0.0, -1.0,
                                            ALU.is_gt, ALU.add).then_inc(adj_turned, 1)

                def diff_of(t, k):
                    u = KU * t + k
                    nc.vector.tensor_scalar(bias_rhs[0:KC, k % 2, :], c_rows[:, :], c_cols[:, bass.ds(u, 1)], 0.0,
                                            ALU.subtract, ALU.max).then_inc(diff_ready, 1)

                def max_of(t, k, first=False):
                    u = KU * t + k
                    if not first:
                        dve.wait_ge(probs_ready, u)
                    dve.wait_ge(relu_ready, u + 1)
                    dve.wait_ge(logits_ready, u + 1)
                    nc.vector.memset(waited[:, :], 0.0)
                    nc.vector.tensor_tensor_reduce(out=logits[:, :], in0=psL[:, :], in1=relu_part[:, :],
                                                   scale=1.0, scalar=-3.0e38, op0=ALU.add, op1=ALU.max,
                                                   accum_out=mx[:, :]).then_inc(mx_found, 1)
                    dve.wait_ge(mx_found, u + 1)
                    nc.vector.tensor_scalar(neg_mx[:, :], mx[:, :], -1.0, None, ALU.mult).then_inc(mx_ready, 1)

                def pick(t, k):
                    u = KU * t + k
                    dve.wait_ge(pv_ready, u + 1)
                    nc.vector.reciprocal(rinv[:, k % 2:k % 2 + 1], rsum[:, k % 2:k % 2 + 1]).then_inc(rinv_ready, 1)
                    dve.wait_ge(rinv_ready, u + 1)
                    nc.vector.scalar_tensor_tensor(picked[:, k % 2, :], psV[:, k % 2, :], rinv[:, k % 2:k % 2 + 1],
                                                   own_head[:, :], ALU.mult, ALU.mult).then_inc(picked_ready, 1)

                def choose(t, k):
                    v = H * t + k
                    dve.wait_ge(sim_copied, v + 1)
                    dve.sem_inc(sim_seen, 1)
                    s = sim[:, k % 2, :, :]
                    first = [c.did(nc.vector.max(best[:, p, 0:8], s[:, p, :])) for p in range(2)]
                    removed = []
                    for p in range(2):
                        dve.wait_ge(step, first[p])
                        removed.append(c.did(nc.vector.match_replace(rest[:, p, :], best[:, p, 0:8], s[:, p, :],
                                                                     LOWEST)))
                    for p in range(2):
                        c.did(nc.vector.max_index(best_at[:, p, 0:8], best[:, p, 0:8], s[:, p, :]))
                    second = []
                    for p in range(2):
                        dve.wait_ge(step, removed[p])
                        second.append(c.did(nc.vector.max(best[:, p, 8:16], rest[:, p, :])))
                    for p in range(2):
                        dve.wait_ge(step, second[p])
                        found = c.did(nc.vector.max_index(best_at[:, p, 8:16], best[:, p, 8:16], rest[:, p, :]))
                    at = 0
                    spans = []
                    for i, n, m in RUNS:
                        spans.append((at, i, n, m))
                        at += n * m
                    for at, i, n, m in spans:
                        summed = c.did(nc.vector.tensor_tensor(
                            cand[:, at:at + n * m].rearrange("p (a b) -> p a b", b=m),
                            best[:, 0, i:i + n].unsqueeze(2).to_broadcast([P, n, m]),
                            best[:, 1, 0:m].unsqueeze(1).to_broadcast([P, n, m]), ALU.add))
                    dve.wait_ge(step, found)
                    c.did(nc.vector.tensor_scalar(at0[:, :], best_at[:, 0, :], float(k * NK * NK), None, ALU.add))
                    placed = c.did(nc.vector.tensor_scalar(at1[:, :], best_at[:, 1, :], float(NK), None, ALU.mult))
                    dve.wait_ge(step, summed)
                    t1 = c.did(nc.vector.max(top[:, 0:8], cand[:, :]))
                    dve.wait_ge(step, placed)
                    for at, i, n, m in spans:
                        numbered = c.did(nc.vector.tensor_tensor(
                            cand_row[:, at:at + n * m].rearrange("p (a b) -> p a b", b=m),
                            at0[:, i:i + n].unsqueeze(2).to_broadcast([P, n, m]),
                            at1[:, 0:m].unsqueeze(1).to_broadcast([P, n, m]), ALU.add))
                    dve.wait_ge(step, t1)
                    t2 = c.did(nc.vector.match_replace(cand_rest[:, :], top[:, 0:8], cand[:, :], LOWEST))
                    c.did(nc.vector.max_index(top_at[:, 0:8], top[:, 0:8], cand[:, :]))
                    dve.wait_ge(step, t2)
                    t3 = c.did(nc.vector.max(top[:, 8:16], cand_rest[:, :]))
                    dve.wait_ge(step, t3)
                    nc.vector.tensor_scalar(neg_top[:, :], top[:, 0:1], -1.0, None, ALU.mult).then_inc(top_ready, 1)
                    t4 = c.did(nc.vector.max_index(top_at[:, 8:16], top[:, 8:16], cand_rest[:, :]))
                    dve.wait_ge(step, t4)
                    t5 = c.did(nc.vector.tensor_tensor(hit[:, :, :],
                                                       top_at[:, :].unsqueeze(2).to_broadcast([P, TOP, CAND]),
                                                       cand_no[:, :].unsqueeze(1).to_broadcast([P, TOP, CAND]),
                                                       ALU.is_equal))
                    dve.wait_ge(step, t5)
                    t6 = c.did(nc.vector.tensor_tensor(hit[:, :, :], hit[:, :, :],
                                                       cand_row[:, :].unsqueeze(1).to_broadcast([P, TOP, CAND]),
                                                       ALU.mult))
                    dve.wait_ge(step, t6)
                    with nc.allow_low_precision(reason="whole numbers below 2**24, one of them not zero"):
                        c.did(nc.vector.tensor_reduce(rows[:, k, :], hit[:, :, :], mybir.AxisListType.X, ALU.add))
                    c.restart()
                    dve.sem_inc(rows_ready, 1)
                    dve.sem_inc(sim_free, 1)
                    dve.wait_ge(exp_ready, v + 1)
                    n1 = c.did(nc.vector.reciprocal(inv_w[:, k:k + 1], sum_w[:, k:k + 1]))
                    c.restart()

                def add_up(t, k, after_first):
                    u = H * t + k
                    done = []
                    for s in range(TOP):
                        slot = (k % 2) * TOP + s
                        dve.wait_ge(got[slot], 16 * ((H // 2) * t + k // 2 + 1))
                        if s >= 2:
                            dve.wait_ge(step, done[s - 2])
                            done.append(c.did(nc.vector.scalar_tensor_tensor(
                                part[:, s % 2, :], ring[:, slot, :], raw_w[:, k, s:s + 1],
                                part[:, s % 2, :], ALU.mult, ALU.add)))
                        else:
                            done.append(c.did(nc.vector.tensor_scalar(
                                part[:, s % 2, :], ring[:, slot, :], raw_w[:, k, s:s + 1], None, ALU.mult)))
                    dve.wait_ge(step, done[TOP - 1])
                    both = c.did(nc.vector.tensor_tensor(part[:, 0, :], part[:, 0, :],
                                                         part[:, 1, :], ALU.add))
                    dve.wait_ge(step, both)
                    if after_first:
                        dve.wait_ge(key_turned, u)
                    if k == 0:
                        dve.wait_ge(values_tile_free, t + 1)
                    c.did(nc.vector.tensor_scalar(total[:, :], part[:, 0, 0:C], inv_w[:, k:k + 1], None,
                                                  ALU.mult))
                    c.did(nc.vector.tensor_scalar(values_tile[:, k, :], part[:, 0, C:2 * C], inv_w[:, k:k + 1],
                                                  None, ALU.mult))
                    c.restart()
                    dve.sem_inc(total_ready, 1)
                    dve.sem_inc(ring_free, 1)

                def tile(t, s1, last, choosing, adding):
                    for k in range(H):
                        ahead = k < KU - 1 or not last
                        if s1 and (k < KU - 2 or not last):
                            diff_of(t, k + 2)
                        if s1 and k == KU - 1 and not last:
                            turn_adj(t + 1)
                        if adding:
                            add_up(t - 2, k, after_first=k >= 1)
                        if s1 and ahead:
                            max_of(t + (k + 1) // KU, (k + 1) % KU)
                        if choosing:
                            choose(t - 1, k)
                        if s1:
                            pick(t, k)
                    if s1:
                        dve.wait_ge(folded, t + 1)
                        nc.vector.tensor_tensor(X[:, t, :], X[:, t, :], psO[:, 0:P], ALU.add).then_inc(x_added, 1)
                        dve.wait_ge(x_added, t + 1)
                        nc.vector.memset(waited[:, :], 0.0)
                        nc.vector.bn_stats(row_stats[:, :], X[:, t, :]).then_inc(stats_ready, 1)
                        dve.wait_ge(stats_ready, t + 1)
                        nc.vector.memset(waited[:, :], 0.0)
                        nc.vector.bn_aggr(row_mv[:, :], row_stats[:, :]).then_inc(moments_ready, 1)
                        dve.wait_ge(std_ready, t + 1)
                        nc.vector.reciprocal(row_rstd[:, :], row_std[:, :]).then_inc(rstd_ready, 1)
                        dve.wait_ge(rstd_ready, t + 1)
                        nc.vector.tensor_scalar(row_xn[:, :], X[:, t, :], row_mv[:, 0:1], row_rstd[:, :],
                                                ALU.subtract, ALU.mult).then_inc(xn_ready, 1)

                turn_adj(0)
                diff_of(0, 0)
                diff_of(0, 1)
                dve.wait_ge(keys_in, 64)
                max_of(0, 0, first=True)
                each_tile(dve, tile)


def causal_attention(nc, ins, X, keysT_in, values_in, ident, big_ident, psL, psT, psV, psO):
    fp32 = mybir.dt.float32
    bf16 = mybir.dt.bfloat16
    ALU = mybir.AluOpType
    ACT = mybir.ActivationFunctionType
    TC = CH // P
    with ExitStack() as ctx:
        def sb(name, shape, dt=fp32):
            return ctx.enter_context(nc.sbuf_tensor("at_" + name, shape, dt))

        sem = stage_semaphores(nc, ctx, "at_")

        keysT = sb("keysT", [P, T, H, C])
        values = sb("values", [P, T, H, C])
        xT = sb("xT", [P, N])
        wq = sb("wq", [P, H, C])
        wo = sb("wo", [P, H, C])
        ahead = sb("ahead", [P, TC, CH], bf16)
        qT = sb("qT", [P, H, P])
        probs = sb("probs", [P, 2, N])
        probsT = sb("probsT", [P, T, P])
        neg_mx = sb("neg_mx", [P, 2])
        rsum = sb("rsum", [P, 2])
        rinv = sb("rinv", [P, 2])
        headT = sb("headT", [P, 2, P])
        norm = Norm(nc, ctx, "at_norm", X, xT[:, :], probsT, ident, psT)

        consts_in = sem("consts_in")
        chunk_in = [sem(f"chunk_in{g}") for g in range(NC)]
        q_done = sem("q_done")
        q_ready = sem("q_ready")
        logits_ready = sem("logits_ready")
        mx_ready = sem("mx_ready")
        probs_ready = sem("probs_ready")
        turned = sem("turned")
        probsT_ready = sem("probsT_ready")
        pv_ready = sem("pv_ready")
        head_ready = sem("head_ready")
        out_done = sem("out_done")
        rinv_ready = sem("rinv_ready")
        x_added = sem("x_added")

        with nc.Block() as block:
            @block.sync
            def _(sp):
                sp.dma_start(wq[:, :, :], ins["Wq"]).then_inc(consts_in, 16)
                sp.dma_start(wo[:, :, :], ins["Wo"]).then_inc(consts_in, 16)
                sp.dma_start(ahead[:, :, :], ins["c_ahead"]).then_inc(consts_in, 16)
                for g in range(NC):
                    for t in range(g * TC, (g + 1) * TC):
                        sp.dma_start(keysT[:, t, :, :], keysT_in[t, :, :, :]).then_inc(chunk_in[g], 16)
                        sp.dma_start(values[:, t, :, :], values_in[t, :, :, :]).then_inc(chunk_in[g], 16)

            @block.tensor
            def _(pe):
                norm.tensor(pe)
                pe.wait_ge(norm.xT_done, T // 4)
                pe.wait_ge(consts_in, 48)

                def logits_of(t, r, k, chunks):
                    u = H * t + k
                    for c in range(chunks):
                        diagonal = c == chunks - 1
                        nc.tensor.matmul(psL[:, c * CH:(c + 1) * CH], qT[:, k, :], keysT[:, c * TC:(c + 1) * TC, k, :],
                                         start=True, stop=not diagonal)
                    nc.tensor.matmul(psL[:, c * CH:(c + 1) * CH], big_ident[:, :], ahead[:, r, :],
                                     start=False, stop=True).then_inc(logits_ready, 1)

                def turn(k, q):
                    for s in range(4):
                        j = 4 * q + s
                        last = nc.tensor.transpose(psT[:, q % 2, s * P:(s + 1) * P],
                                                   probs[:, k % 2, j * P:(j + 1) * P], ident[:, :])
                    last.then_inc(turned, 1)

                def weigh(n, k, q, chunks):
                    pe.wait_ge(probsT_ready, n)
                    for s in range(4):
                        j = 4 * q + s
                        last = nc.tensor.matmul(psV[:, k % 2, :], values[:, j, k, :], probsT[:, j, :],
                                                start=(j == 0), stop=(j == 4 * chunks - 1))
                    if q == chunks - 1:
                        last.then_inc(pv_ready, 1)

                def project(t, k):
                    u = H * t + k
                    pe.wait_ge(head_ready, u + 1)
                    nc.tensor.matmul(psO[:, (k % 2) * P:(k % 2) * P + P], headT[:, k % 2, :], wo[:, k, :],
                                     start=True, stop=True).then_inc(out_done, 1)

                def tile(t, r, blocks_before, chunks):
                    for k in range(H):
                        nc.tensor.matmul(psT[:, k // 4, (k % 4) * P:(k % 4 + 1) * P], wq[:, k, :],
                                         xT[:, bass.ts(t, P)], start=True, stop=True).then_inc(q_done, 1)
                    pe.wait_ge(q_ready, 2 * t + 2)
                    logits_of(t, r, 0, chunks)
                    for k in range(H):
                        u = H * t + k
                        pe.wait_ge(probs_ready, u + 1)
                        if k < H - 1:
                            logits_of(t, r, k + 1, chunks)
                        n = blocks_before + k * chunks
                        turn(k, 0)
                        if k >= 1:
                            project(t, k - 1)
                        for q in range(chunks):
                            if q + 1 < chunks:
                                turn(k, q + 1)
                            weigh(n + q + 1, k, q, chunks)
                    project(t, H - 1)

                for g in range(NC):
                    pe.wait_ge(chunk_in[g], 16 * 2 * TC)
                    with pe.Fori(0, TC) as r:
                        tile(r + g * TC, r, H * TC * (g * (g + 1) // 2) + r * (H * (g + 1)), g + 1)

            @block.scalar
            def _(act):
                norm.scalar(act)

                def exp_of(t, k, chunks):
                    act.wait_ge(mx_ready, H * t + k + 1)
                    nc.scalar.activation(probs[:, k % 2, 0:chunks * CH], psL[:, 0:chunks * CH], ACT.Exp,
                                         bias=neg_mx[:, k % 2:k % 2 + 1],
                                         accum_out=rsum[:, k % 2:k % 2 + 1]).then_inc(probs_ready, 1)

                def tile(t, r, blocks_before, chunks):
                    for b in range(2):
                        act.wait_ge(q_done, H * t + 4 * b + 4)
                        nc.scalar.mul(qT[:, 4 * b:4 * b + 4, :].rearrange("p s c -> p (s c)"), psT[:, b, :],
                                      float(C) ** -0.5).then_inc(q_ready, 1)
                    exp_of(t, 0, chunks)
                    for k in range(H):
                        for q in range(chunks):
                            act.wait_ge(turned, blocks_before + k * chunks + q + 1)
                            nc.scalar.copy(probsT[:, 4 * q:4 * q + 4, :].rearrange("p s c -> p (s c)"),
                                           psT[:, q % 2, :]).then_inc(probsT_ready, 1)
                        if k < H - 1:
                            exp_of(t, k + 1, chunks)

                for g in range(NC):
                    with act.Fori(0, TC) as r:
                        tile(r + g * TC, r, H * TC * (g * (g + 1) // 2) + r * (H * (g + 1)), g + 1)

            @block.vector
            def _(dve):
                norm.vector(dve)

                def max_of(t, k, chunks):
                    dve.wait_ge(logits_ready, H * t + k + 1)
                    nc.vector.tensor_reduce(neg_mx[:, k % 2:k % 2 + 1], psL[:, 0:chunks * CH],
                                            mybir.AxisListType.X, ALU.max, negate=True).then_inc(mx_ready, 1)

                def head_of(t, k):
                    dve.wait_ge(pv_ready, H * t + k + 1)
                    nc.vector.tensor_copy(headT[:, k % 2, :], psV[:, k % 2, :]).then_inc(head_ready, 1)
                    nc.vector.reciprocal(rinv[:, k % 2:k % 2 + 1], rsum[:, k % 2:k % 2 + 1]).then_inc(rinv_ready, 1)

                def add_head(t, k):
                    u = H * t + k
                    dve.wait_ge(rinv_ready, u + 1)
                    dve.wait_ge(out_done, u + 1)
                    nc.vector.scalar_tensor_tensor(X[:, t, :], psO[:, (k % 2) * P:(k % 2) * P + P],
                                                   rinv[:, k % 2:k % 2 + 1], X[:, t, :],
                                                   ALU.mult, ALU.add).then_inc(x_added, 1)

                def tile(t, chunks):
                    max_of(t, 0, chunks)
                    for k in range(H):
                        if k < H - 1:
                            max_of(t, k + 1, chunks)
                        if k >= 1:
                            add_head(t, k - 1)
                        head_of(t, k)
                    add_head(t, H - 1)

                for g in range(NC):
                    with dve.Fori(0, TC) as r:
                        tile(r + g * TC, g + 1)


def graph_attention(nc, ins, X, adj_neg, ident, big_ident, psL, psT, psV, psO):
    fp32 = mybir.dt.float32
    bf16 = mybir.dt.bfloat16
    ALU = mybir.AluOpType
    ACT = mybir.ActivationFunctionType
    SLOPE = 0.2
    with ExitStack() as ctx:
        def sb(name, shape, dt=fp32):
            return ctx.enter_context(nc.sbuf_tensor("ga_" + name, shape, dt))

        sem = stage_semaphores(nc, ctx, "ga_")

        vals = sb("vals", [P, T, H, C])
        w_out = sb("w_out", [P, H, C])
        b_out = sb("b_out", [P, C])
        s1_cols = sb("s1_cols", [P, T, H])
        s2_parts = sb("s2_parts", [3 * 32, N], bf16)
        s2_pick = sb("s2_pick", [3 * 32, H, P], bf16)
        relu_part = sb("relu_part", [P, N])
        logits = sb("logits", [P, N])
        probs = sb("probs", [P, N])
        probsT = sb("probsT", [P, T, P])
        mx = sb("mx", [P, 1])
        waited = sb("waited", [P, 1])
        neg_mx = sb("neg_mx", [P, 1])
        rsum = sb("rsum", [P, 1])
        rinv = sb("rinv", [P, 1])
        above = sb("above", [P, P])
        below = sb("below", [P, P])
        exp_below = sb("exp_below", [P, P])
        feat = sb("feat", [P, P])
        featT = sb("featT", [P, P])
        xT = logits
        w_all = relu_part[:, 0:H * C]
        w_heads_t = relu_part[:, H * C:2 * H * C].rearrange("d (h f) -> d h f", h=H)
        a_cols = probs[:, 0:2 * H]
        wa = probs[:, 64:64 + 2 * H]
        s2_rows = relu_part[0:H, :]
        s2_rest = probs[0:H, :]
        norm = Norm(nc, ctx, "ga_norm", X, xT[:, :], probsT, ident, psT)

        consts_in = sem("consts_in")
        wa_done = sem("wa_done")
        wa_copied = sem("wa_copied")
        vals_done = sem("vals_done")
        vals_copied = sem("vals_copied")
        s1_done = sem("s1_done")
        s2_done = sem("s2_done")
        s1_copied = sem("s1_copied")
        zeroed = sem("zeroed")
        split = sem("split")
        moved = sem("moved")
        logits_ready = sem("logits_ready")
        logits_seen = sem("logits_seen")
        relu_ready = sem("relu_ready")
        mx_found = sem("mx_found")
        mx_ready = sem("mx_ready")
        probs_ready = sem("probs_ready")
        turned = sem("turned")
        probsT_dve = sem("probsT_dve")
        probsT_act = sem("probsT_act")
        pv_ready = sem("pv_ready")
        rinv_ready = sem("rinv_ready")
        below_ready = sem("below_ready")
        exp_ready = sem("exp_ready")
        feat_ready = sem("feat_ready")
        feat_turned = sem("feat_turned")
        featT_ready = sem("featT_ready")
        projected = sem("projected")
        x_added = sem("x_added")

        with nc.Block() as block:
            @block.sync
            def _(sp):
                sp.dma_start(w_all, ins["W_all"]).then_inc(consts_in, 16)
                sp.dma_start(w_heads_t, ins["W_heads_t"]).then_inc(consts_in, 16)
                sp.dma_start(a_cols, ins["a_cols"]).then_inc(consts_in, 16)
                sp.dma_start(w_out[:, :, :], ins["W_out"]).then_inc(consts_in, 16)
                sp.dma_start(b_out[:, :], ins["b_out"].to_broadcast([P, C])).then_inc(consts_in, 16)
                sp.dma_start(s2_pick[:, :, :], ins["c_s2_pick"]).then_inc(consts_in, 16)

            @block.tensor
            def _(pe):
                norm.tensor(pe)
                pe.wait_ge(consts_in, 96)
                for a in range(2):
                    for k in range(H):
                        n = a * H + k
                        last = nc.tensor.matmul(psO[:, n:n + 1], w_heads_t[:, k, :], a_cols[:, n:n + 1],
                                                start=True, stop=True)
                last.then_inc(wa_done, 1)
                pe.wait_ge(norm.xT_done, T // 4)
                for t in range(T):
                    if t >= 2:
                        pe.wait_ge(vals_copied, t - 1)
                    for b in range(2):
                        last = nc.tensor.matmul(psL[:, (2 * (t % 2) + b) * CH:(2 * (t % 2) + b + 1) * CH],
                                                xT[:, t * P:(t + 1) * P], w_all[:, b * CH:(b + 1) * CH],
                                                start=True, stop=True)
                    last.then_inc(vals_done, 1)
                pe.wait_ge(wa_copied, 1)
                for t in range(T):
                    last = nc.tensor.matmul(psO[:, t * H:(t + 1) * H], xT[:, t * P:(t + 1) * P], wa[:, 0:H],
                                            start=True, stop=True)
                last.then_inc(s1_done, 1)
                pe.wait_ge(vals_copied, T)
                for c in range(NC):
                    last = nc.tensor.matmul(psL[0:H, c * CH:(c + 1) * CH], wa[:, H:2 * H],
                                            xT[:, c * CH:(c + 1) * CH], start=True, stop=True)
                last.then_inc(s2_done, 1)

                def logits_of(t, k, first=False):
                    for c in range(NC):
                        if c == 0 and not first:
                            pe.wait_ge(mx_ready, H * t + k)
                        nc.tensor.matmul(psL[:, c * CH:(c + 1) * CH], big_ident[:, :],
                                         adj_neg[:, t, c * CH:(c + 1) * CH], start=True, stop=False)
                        last = nc.tensor.matmul(psL[:, c * CH:(c + 1) * CH], s2_pick[:, k, :],
                                                s2_parts[:, c * CH:(c + 1) * CH], start=False, stop=True)
                    last.then_inc(logits_ready, 1)

                def turn(q):
                    for s in range(4):
                        j = 4 * q + s
                        last = nc.tensor.transpose(psT[:, q % 2, s * P:(s + 1) * P],
                                                   probs[:, j * P:(j + 1) * P], ident[:, :])
                    last.then_inc(turned, 1)

                def weigh(t, k, q):
                    u = H * t + k
                    if q < 2:
                        pe.wait_ge(probsT_dve, 2 * u + q + 1)
                    else:
                        pe.wait_ge(probsT_act, 2 * u + q - 1)
                    for s in range(4):
                        j = 4 * q + s
                        last = nc.tensor.matmul(psV[:, 0, :], probsT[:, j, :], vals[:, j, k, :],
                                                start=(j == 0), stop=(j == T - 1))
                    if q == 3:
                        last.then_inc(pv_ready, 1)

                def turn_feat(t, k):
                    pe.wait_ge(feat_ready, H * t + k + 1)
                    nc.tensor.transpose(psV[:, 1, :], feat[:, :], ident[:, :]).then_inc(feat_turned, 1)

                def project(t, k):
                    pe.wait_ge(featT_ready, H * t + k + 1)
                    last = nc.tensor.matmul(psO[:, 0:C], featT[:, :], w_out[:, k, :],
                                            start=(k == 0), stop=(k == H - 1))
                    if k == H - 1:
                        last.then_inc(projected, 1)

                def tile(t, last):
                    for k in range(H):
                        if k < H - 1:
                            logits_of(t, k + 1)
                        elif not last:
                            logits_of(t + 1, 0)
                        if k >= 1:
                            turn_feat(t, k - 1)
                        pe.wait_ge(probs_ready, H * t + k + 1)
                        turn(0)
                        turn(1)
                        if k >= 1:
                            project(t, k - 1)
                        weigh(t, k, 0)
                        turn(2)
                        weigh(t, k, 1)
                        turn(3)
                        weigh(t, k, 2)
                        weigh(t, k, 3)
                    turn_feat(t, H - 1)
                    project(t, H - 1)

                pe.wait_ge(split, 5)
                pe.wait_ge(s1_copied, 1)
                logits_of(0, 0, first=True)
                with pe.Fori(0, T - 1) as t:
                    tile(t, False)
                tile(T - 1, True)

            @block.scalar
            def _(act):
                norm.scalar(act)
                act.wait_ge(wa_done, 1)
                nc.scalar.copy(wa, psO[:, 0:2 * H]).then_inc(wa_copied, 1)
                for t in range(T):
                    act.wait_ge(vals_done, t + 1)
                    nc.scalar.copy(vals[:, t, :, :].rearrange("p h c -> p (h c)"),
                                   psL[:, (t % 2) * 2 * CH:(t % 2 + 1) * 2 * CH]).then_inc(vals_copied, 1)
                act.wait_ge(s1_done, 1)
                nc.scalar.mul(s1_cols[:, :, :].rearrange("p t h -> p (t h)"), psO[:, 0:T * H],
                              1.0 - SLOPE).then_inc(s1_copied, 1)
                act.wait_ge(s1_copied, 1)

                def relu_of(t, k):
                    act.wait_ge(logits_ready, H * t + k + 1)
                    act.sem_inc(logits_seen, 1)
                    nc.scalar.activation(relu_part[:, :], psL[:, :], ACT.Relu, bias=s1_cols[:, t, k:k + 1],
                                         scale=(1.0 - SLOPE) / SLOPE).then_inc(relu_ready, 1)

                def exp_of(t, k):
                    act.wait_ge(mx_ready, H * t + k + 1)
                    nc.scalar.activation(probs[:, :], logits[:, :], ACT.Exp, bias=neg_mx[:, :],
                                         accum_out=rsum[:, :]).then_inc(probs_ready, 1)

                def copy_turned(t, k, q):
                    act.wait_ge(turned, 4 * (H * t + k) + q + 1)
                    nc.scalar.copy(probsT[:, 4 * q:4 * q + 4, :].rearrange("p s c -> p (s c)"),
                                   psT[:, q % 2, :]).then_inc(probsT_act, 1)

                def exp_below_of(t, k):
                    act.wait_ge(below_ready, H * t + k + 1)
                    nc.scalar.activation(exp_below[:, :], below[:, :], ACT.Exp).then_inc(exp_ready, 1)

                def keep_featT(t, k):
                    act.wait_ge(feat_turned, H * t + k + 1)
                    nc.scalar.copy(featT[:, :], psV[:, 1, :]).then_inc(featT_ready, 1)

                def tile(t, last):
                    for k in range(H):
                        if k >= 1:
                            keep_featT(t, k - 1)
                        if k < H - 1 or not last:
                            relu_of(t + (k + 1) // H, (k + 1) % H)
                        copy_turned(t, k, 2)
                        copy_turned(t, k, 3)
                        if k < H - 1 or not last:
                            exp_of(t + (k + 1) // H, (k + 1) % H)
                        exp_below_of(t, k)
                    keep_featT(t, H - 1)

                act.wait_ge(split, 5)
                relu_of(0, 0)
                exp_of(0, 0)
                with act.Fori(0, T - 1) as t:
                    tile(t, False)
                tile(T - 1, True)

            @block.vector
            def _(dve):
                norm.vector(dve)
                nc.vector.memset(s2_parts[:, :], 0.0).then_inc(zeroed, 1)
                dve.wait_ge(zeroed, 1)
                dve.wait_ge(vals_copied, T)
                dve.wait_ge(s2_done, 1)
                dve.wait_ge(s1_done, 1)
                nc.vector.tensor_scalar(s2_rows, psL[0:H, :], SLOPE, None, ALU.mult).then_inc(split, 1)
                dve.wait_ge(split, 1)
                nc.vector.tensor_copy(s2_parts[0:H, :], s2_rows).then_inc(split, 1)
                dve.wait_ge(split, 2)
                nc.vector.tensor_tensor(s2_rest, s2_rows, s2_parts[0:H, :], ALU.subtract).then_inc(split, 1)
                dve.wait_ge(split, 3)
                nc.vector.tensor_copy(s2_parts[32:32 + H, :], s2_rest).then_inc(split, 1)
                dve.wait_ge(split, 4)
                nc.vector.tensor_copy(s2_rows, s2_parts[32:32 + H, :]).then_inc(moved, 1)
                dve.wait_ge(moved, 1)
                nc.vector.tensor_tensor(s2_parts[64:64 + H, :], s2_rest, s2_rows, ALU.subtract).then_inc(split, 1)

                def copy_turned(t, k, q):
                    dve.wait_ge(turned, 4 * (H * t + k) + q + 1)
                    nc.vector.tensor_copy(probsT[:, 4 * q:4 * q + 4, :].rearrange("p s c -> p (s c)"),
                                          psT[:, q % 2, :]).then_inc(probsT_dve, 1)

                def max_of(t, k):
                    u = H * t + k
                    dve.wait_ge(relu_ready, u + 1)
                    nc.vector.memset(waited[:, :], 0.0)
                    nc.vector.tensor_tensor_reduce(out=logits[:, :], in0=psL[:, :], in1=relu_part[:, :],
                                                   scale=1.0, scalar=-3.0e38, op0=ALU.add, op1=ALU.max,
                                                   accum_out=mx[:, :]).then_inc(mx_found, 1)
                    dve.wait_ge(mx_found, u + 1)
                    nc.vector.tensor_scalar(neg_mx[:, :], mx[:, :], -1.0, None, ALU.mult).then_inc(mx_ready, 1)

                def elu_of(t, k):
                    u = H * t + k
                    dve.wait_ge(rinv_ready, u + 1)
                    dve.wait_ge(pv_ready, u + 1)
                    nc.vector.tensor_scalar(above[:, :], psV[:, 0, :], rinv[:, :], 0.0, ALU.mult, ALU.max)
                    nc.vector.tensor_scalar(below[:, :], psV[:, 0, :], rinv[:, :], 0.0, ALU.mult, ALU.min
                                            ).then_inc(below_ready, 1)
                    dve.wait_ge(exp_ready, u + 1)
                    nc.vector.scalar_tensor_tensor(feat[:, :], exp_below[:, :], -1.0, above[:, :],
                                                   ALU.add, ALU.add).then_inc(feat_ready, 1)

                def sum_of(t, k):
                    dve.wait_ge(probs_ready, H * t + k + 1)
                    nc.vector.reciprocal(rinv[:, :], rsum[:, :]).then_inc(rinv_ready, 1)

                def tile(t, last):
                    for k in range(H):
                        sum_of(t, k)
                        copy_turned(t, k, 0)
                        copy_turned(t, k, 1)
                        if k < H - 1 or not last:
                            max_of(t + (k + 1) // H, (k + 1) % H)
                        elu_of(t, k)
                    dve.wait_ge(projected, t + 1)
                    nc.vector.tensor_tensor(X[:, t, :], X[:, t, :], psO[:, 0:C], ALU.add).then_inc(x_added, 1)
                    dve.wait_ge(x_added, 2 * t + 1)
                    nc.vector.tensor_tensor(X[:, t, :], X[:, t, :], b_out[:, :], ALU.add).then_inc(x_added, 1)

                max_of(0, 0)
                with dve.Fori(0, T - 1) as t:
                    tile(t, False)
                tile(T - 1, True)


def experts(nc, ins, X, ident, psL, psT, psO):
    fp32 = mybir.dt.float32
    u32 = mybir.dt.uint32
    ALU = mybir.AluOpType
    ACT = mybir.ActivationFunctionType
    E = 16
    F = 256
    FH = F // P
    TC = CH // P
    with ExitStack() as ctx:
        def sb(name, shape, dt=fp32):
            return ctx.enter_context(nc.sbuf_tensor("ex_" + name, shape, dt))

        sem = stage_semaphores(nc, ctx, "ex_")

        w1 = sb("w1", [P, E, F])
        b1 = sb("b1", [P, E, FH])
        w2 = sb("w2", [P, E, FH, C])
        b2 = sb("b2", [E, C])
        gate_w = sb("gate_w", [P, E])
        gate_b = sb("gate_b", [P, E])
        gamma = sb("gamma", [P, C])
        beta = sb("beta", [P, C])
        expert_no = sb("expert_no", [P, E])
        xT = sb("xT", [P, N])
        xn = sb("xn", [P, T, C])
        y = sb("y", [P, T, C])
        gates = sb("gates", [P, T, E])
        best = sb("best", [P, T, 8])
        best_at = sb("best_at", [P, T, 8], u32)
        gap = sb("gap", [P, T])
        second = sb("second", [P, T])
        both = sb("both", [P, T])
        share = sb("share", [P, 2, T])
        at_best = sb("at_best", [P, 2, T, E])
        wgt = sb("wgt", [P, T, E])
        wgtT = sb("wgtT", [E, N])
        hid = sb("hid", [P, 2, FH, CH])
        stats = sb("stats", [P, T, 6])
        mv = sb("mv", [P, T, 2])
        eps = sb("eps", [P, 1])
        std = sb("std", [P, T])
        norm = Norm(nc, ctx, "ex_norm", X, xT[:, :], xn, ident, psT)

        consts_in = sem("consts_in")
        gates_done = sem("gates_done")
        step = sem("step")
        gap_ready = sem("gap_ready")
        second_ready = sem("second_ready")
        wgt_ready = sem("wgt_ready")
        wgt_turned = sem("wgt_turned")
        wgtT_ready = sem("wgtT_ready")
        b2_done = sem("b2_done")
        b2_added = sem("b2_added")
        up_done = sem("up_done")
        hid_ready = sem("hid_ready")
        down_done = sem("down_done")
        bank_free = sem("bank_free")
        y_added = sem("y_added")
        moments = sem("moments")
        std_done = sem("std_done")
        finished = sem("finished")

        with nc.Block() as block:
            @block.sync
            def _(sp):
                sp.dma_start(w1[:, :, :], ins["w1"]).then_inc(consts_in, 16)
                sp.dma_start(w2[:, :, :, :], ins["w2"]).then_inc(consts_in, 16)
                sp.dma_start(b1[:, :, :], ins["b1"]).then_inc(consts_in, 16)
                sp.dma_start(b2[:, :], ins["b2"]).then_inc(consts_in, 16)
                sp.dma_start(gate_w[:, :], ins["gate_w"]).then_inc(consts_in, 16)
                sp.dma_start(gate_b[:, :], ins["gate_b"].to_broadcast([P, E])).then_inc(consts_in, 16)
                sp.dma_start(gamma[:, :], ins["gamma"].to_broadcast([P, C])).then_inc(consts_in, 16)
                sp.dma_start(beta[:, :], ins["beta"].to_broadcast([P, C])).then_inc(consts_in, 16)
                sp.dma_start(expert_no[:, :], ins["c_expert_no"]).then_inc(consts_in, 16)

            @block.tensor
            def _(pe):
                norm.tensor(pe)
                pe.wait_ge(consts_in, 144)
                pe.wait_ge(norm.xT_done, T // 4)
                for t in range(T):
                    last = nc.tensor.matmul(psO[:, t * E:(t + 1) * E], xT[:, t * P:(t + 1) * P], gate_w[:, :],
                                            start=True, stop=True)
                last.then_inc(gates_done, 1)
                pe.wait_ge(wgt_ready, 1)
                for t in range(T):
                    last = nc.tensor.transpose(psL[0:E, t * P:(t + 1) * P], wgt[:, t, :], ident[:, :])
                last.then_inc(wgt_turned, 1)
                pe.wait_ge(wgtT_ready, 1)
                for t in range(T):
                    last = nc.tensor.matmul(psL[:, t * P:(t + 1) * P], wgtT[:, t * P:(t + 1) * P], b2[:, :],
                                            start=True, stop=True)
                last.then_inc(b2_done, 1)
                pe.wait_ge(b2_added, 1)

                def up(c, e):
                    for f in range(FH):
                        b = FH * (e % 2) + f
                        last = nc.tensor.matmul(psL[:, b * CH:(b + 1) * CH], w1[:, e, f * P:(f + 1) * P],
                                                xT[:, bass.ts(c, CH)], start=True, stop=True)
                    last.then_inc(up_done, 1)

                def down(c, e):
                    v = E * c + e
                    pe.wait_ge(hid_ready, v + 1)
                    pe.wait_ge(bank_free, v + 1)
                    for s in range(TC):
                        for f in range(FH):
                            last = nc.tensor.matmul(psT[:, e % 2, s * P:(s + 1) * P],
                                                    hid[:, e % 2, f, s * P:(s + 1) * P], w2[:, e, f, :],
                                                    start=(f == 0), stop=(f == FH - 1))
                    last.then_inc(down_done, 1)

                with pe.Fori(0, NC) as c:
                    up(c, 0)
                    for e in range(E):
                        if e < E - 1:
                            up(c, e + 1)
                        down(c, e)

            @block.scalar
            def _(act):
                norm.scalar(act)
                act.wait_ge(gap_ready, 1)
                nc.scalar.activation(second[:, :], gap[:, :], ACT.Exp).then_inc(second_ready, 1)
                act.wait_ge(wgt_turned, 1)
                nc.scalar.copy(wgtT[:, :], psL[0:E, :]).then_inc(wgtT_ready, 1)
                with act.Fori(0, NC) as c:
                    for e in range(E):
                        act.wait_ge(up_done, E * c + e + 1)
                        for f in range(FH):
                            b = FH * (e % 2) + f
                            last = nc.scalar.activation(hid[:, e % 2, f, :], psL[:, b * CH:(b + 1) * CH], ACT.Relu,
                                                        bias=b1[:, e, f:f + 1])
                        last.then_inc(hid_ready, 1)
                act.wait_ge(moments, 1)
                nc.scalar.activation(std[:, :], mv[:, :, 1], ACT.Sqrt, bias=eps[:, :]).then_inc(std_done, 1)

            @block.vector
            def _(dve):
                norm.vector(dve)
                dve.sem_inc(bank_free, 2)
                dve.sem_inc(y_added, TC)
                c = Chain(dve, step)
                nc.vector.memset(eps[:, :], LN_EPS)
                dve.wait_ge(gates_done, 1)
                dve.wait_ge(consts_in, 144)
                a = c.did(nc.vector.tensor_tensor(gates[:, :, :], psO[:, 0:T * E].rearrange("p (t e) -> p t e", e=E),
                                                  gate_b[:, :].unsqueeze(1).to_broadcast([P, T, E]), ALU.add))
                dve.wait_ge(step, a)
                for t in range(T):
                    a = c.did(nc.vector.max(best[:, t, :], gates[:, t, :]))
                dve.wait_ge(step, a)
                for t in range(T):
                    a = c.did(nc.vector.max_index(best_at[:, t, :], best[:, t, :], gates[:, t, :]))
                nc.vector.tensor_tensor(gap[:, :], best[:, :, 1], best[:, :, 0], ALU.subtract).then_inc(gap_ready, 1)
                dve.wait_ge(second_ready, 1)
                a2 = c.did(nc.vector.tensor_scalar(both[:, :], second[:, :], 1.0, None, ALU.add))
                dve.wait_ge(step, a2)
                a3 = c.did(nc.vector.reciprocal(share[:, 0, :], both[:, :]))
                dve.wait_ge(step, a3)
                a4 = c.did(nc.vector.tensor_tensor(share[:, 1, :], share[:, 0, :], second[:, :], ALU.mult))
                dve.wait_ge(step, a4)
                for m in range(2):
                    b = c.did(nc.vector.tensor_tensor(at_best[:, m, :, :],
                                                      best_at[:, :, m:m + 1].to_broadcast([P, T, E]),
                                                      expert_no[:, :].unsqueeze(1).to_broadcast([P, T, E]),
                                                      ALU.is_equal))
                    dve.wait_ge(step, b)
                    b = c.did(nc.vector.tensor_tensor(at_best[:, m, :, :], at_best[:, m, :, :],
                                                      share[:, m, :].unsqueeze(2).to_broadcast([P, T, E]),
                                                      ALU.mult))
                dve.wait_ge(step, b)
                nc.vector.tensor_tensor(wgt[:, :, :], at_best[:, 0, :, :], at_best[:, 1, :, :],
                                        ALU.add).then_inc(wgt_ready, 1)
                dve.wait_ge(b2_done, 1)
                nc.vector.tensor_tensor(y[:, :, :].rearrange("p t c -> p (t c)"), psL[:, :],
                                        xn[:, :, :].rearrange("p t c -> p (t c)"), ALU.add).then_inc(b2_added, 1)
                dve.wait_ge(b2_added, 1)
                with dve.Fori(0, NC) as ch:
                    for e in range(E):
                        v = E * ch + e
                        dve.wait_ge(down_done, v + 1)
                        for s in range(TC):
                            t = TC * ch + s
                            dve.wait_ge(y_added, TC * v + s + 1)
                            last = nc.vector.scalar_tensor_tensor(
                                y[:, t, :], psT[:, e % 2, s * P:(s + 1) * P], wgt[:, t, e:e + 1], y[:, t, :],
                                ALU.mult, ALU.add)
                            last.then_inc(y_added, 1)
                        dve.wait_ge(y_added, TC * v + 2 * TC)
                        dve.sem_inc(bank_free, 1)
                for t in range(T):
                    last = c.did(nc.vector.bn_stats(stats[:, t, :], y[:, t, :]))
                dve.wait_ge(step, last)
                for t in range(T):
                    last = nc.vector.bn_aggr(mv[:, t, :], stats[:, t, :])
                last.then_inc(moments, 1)
                dve.wait_ge(std_done, 1)
                a = c.did(nc.vector.reciprocal(gap[:, :], std[:, :]))
                dve.wait_ge(step, a)
                for t in range(T):
                    a = c.did(nc.vector.tensor_scalar(y[:, t, :], y[:, t, :], mv[:, t, 0:1], gap[:, t:t + 1],
                                                      ALU.subtract, ALU.mult))
                dve.wait_ge(step, a)
                a = c.did(nc.vector.tensor_tensor(y[:, :, :], y[:, :, :],
                                                  gamma[:, :].unsqueeze(1).to_broadcast([P, T, C]), ALU.mult))
                dve.wait_ge(step, a)
                a = c.did(nc.vector.tensor_tensor(y[:, :, :], y[:, :, :],
                                                  beta[:, :].unsqueeze(1).to_broadcast([P, T, C]), ALU.add))
                dve.wait_ge(step, a)
                nc.vector.tensor_tensor(X[:, :, :], X[:, :, :], y[:, :, :], ALU.add).then_inc(finished, 1)
                dve.wait_ge(finished, 1)


def layouts(inputs):
    import numpy as np

    a = {k: np.asarray(v) for k, v in inputs.items()}
    rows = np.arange(P)
    node, head = rows // H, rows % H
    same_node = node[:, None] == np.arange(G)[None, :]
    bias_mask = np.full((KC + NF, P), -1.0, np.float32)
    bias_mask[:KC] = 2.0 * (np.arange(KC)[:, None] // NF == node[None, :])
    k_of = np.arange(P) // G
    i_of = np.arange(P) % G
    spread = (k_of[:, None, None] == np.arange(H)[None, :, None]) & (i_of[:, None, None] == node[None, None, :])
    s2_pick = np.zeros((3 * 32, H, P), np.float32)
    for m in range(3):
        s2_pick[32 * m + np.arange(H), np.arange(H), :] = 1.0
    return {
        "x": a["x"], "adj": a["adj"],
        "c_ident": np.eye(P, dtype=np.float32),
        "c_big_ident": (np.eye(P) * MASKED).astype(np.dtype("bfloat16")),
        "W_t": np.ascontiguousarray(a["L0_gnn_W"].T),
        "a_l": a["L0_gnn_a_l"].reshape(C, 1), "a_r": a["L0_gnn_a_r"].reshape(C, 1),
        "wc_tiled": np.tile(a["L0_gnn_Wc"].T, (G + 1, G)), "gate": a["L0_gnn_gate"].reshape(1, 1),
        "curv_t": np.ascontiguousarray(a["L0_gnn_curv_feats"].T),
        "curv_cols": np.ascontiguousarray(a["L0_gnn_curv_feats"].reshape(N // G, KC).T),
        "c_head_mask": ((rows[:, None] // D0) == head[None, :]).astype(np.float32),
        "c_bias_mask": bias_mask,
        "c_slope_rows": np.float32(0.2) * (np.arange(H)[:, None] == head[None, :]).astype(np.float32),
        "Wq_pk": np.ascontiguousarray(a["L0_ffn_Wq_pk"].reshape(C, 2, H, DK).transpose(0, 2, 1, 3)).reshape(C, H, P),
        "pk_keys": np.ascontiguousarray(a["L0_ffn_pk_keys"].transpose(0, 3, 2, 1)),
        "tables": np.concatenate([a["L0_ffn_keys_table"], a["L0_ffn_values_table"]], axis=1),
        "Wq": a["L0_ffn_Wq"].reshape(C, H, C),
        "Wo": np.ascontiguousarray(a["L0_ffn_Wo"].reshape(H, C, C).transpose(1, 0, 2)),
        "c_cand_no": np.tile(np.arange(CAND, dtype=np.float32), (P, 1)),
        "c_ahead": -(np.arange(CH)[None, None, :] > (P * np.arange(CH // P)[None, :, None] + rows[:, None, None])
                     ).astype(np.dtype("bfloat16")),
        "W_all": np.ascontiguousarray(a["L1_gnn_W_heads"].transpose(1, 0, 2)).reshape(C, H * C),
        "W_heads_t": np.ascontiguousarray(a["L1_gnn_W_heads"].transpose(2, 0, 1)),
        "a_cols": np.ascontiguousarray(np.concatenate([a["L1_gnn_a1"], a["L1_gnn_a2"]]).T),
        "W_out": np.ascontiguousarray(a["L1_gnn_W_out"].reshape(H, C, C).transpose(1, 0, 2)),
        "b_out": a["L1_gnn_b_out"].reshape(1, C),
        "w1": np.ascontiguousarray(a["L1_ffn_w1"].transpose(1, 0, 2)),
        "w2": np.ascontiguousarray(a["L1_ffn_w2"].reshape(16, 2, P, C).transpose(2, 0, 1, 3)),
        "b1": np.ascontiguousarray(a["L1_ffn_b1"].reshape(16, 2, P).transpose(2, 0, 1)),
        "b2": a["L1_ffn_b2"], "gate_w": a["L1_ffn_gate_w"], "gate_b": a["L1_ffn_gate_b"].reshape(1, 16),
        "gamma": a["L1_ffn_gamma"].reshape(1, C), "beta": a["L1_ffn_beta"].reshape(1, C),
        "c_expert_no": np.tile(np.arange(16, dtype=np.float32), (P, 1)),
        "c_s2_pick": s2_pick.astype(np.dtype("bfloat16")),
        "c_spread": (spread * MASKED).astype(np.dtype("bfloat16")),
        "c_fold": np.ascontiguousarray(spread.transpose(2, 1, 0)).astype(np.float32),
        "c_own_head": (head[:, None] == (rows[None, :] // D0)).astype(np.float32),
        "c_node_pick": same_node.astype(np.float32),
    }


def kernel(**inputs):
    import numpy as _np
    import concourse.bacc as _bacc
    from concourse import mybir as _mybir
    from concourse.bass_utils import run_bass_kernel_spmd as _run

    nc = _bacc.Bacc("TRN2", target_bir_lowering=False, num_devices=1)
    arrays, aps = {}, {}
    for name, a in layouts(inputs).items():
        arrays["in_" + name] = a
        aps[name] = nc.dram_tensor("in_" + name, a.shape, _mybir.dt.from_np(a.dtype), kind="ExternalInput").ap()
    out = nc.dram_tensor("out_0", (N, C), _mybir.dt.float32, kind="ExternalOutput").ap()
    program(nc, aps, out)
    r = _run(nc, [arrays], core_ids=[0])
    return r.results[0]["out_0"]
```
